# Optimizing a Trainium2 kernel written in Bass

```python
import numpy as np
import jax
import jax.numpy as jnp

def _softmax(x, axis=-1):
    return jax.nn.softmax(x, axis=axis)

def _gelu(x):
    return jax.nn.gelu(x, approximate=True)

def _silu(x):
    return jax.nn.silu(x)

def _sigmoid(x):
    return jax.nn.sigmoid(x)

def _layernorm(x, axis=-1, eps=1e-05):
    m = jnp.mean(x, axis=axis, keepdims=True)
    v = jnp.var(x, axis=axis, keepdims=True)
    return (x - m) / jnp.sqrt(v + eps)

def _scatter_add(tgt, idx, src, axis=0):
    return tgt.at[idx].add(src)

def _segment_sum(src, seg, n):
    return jax.ops.segment_sum(src, seg, n)
kernel_name = 'mk_perceiver_d1_seqx_r2_1b4c2c'

def setup_inputs(seed: int=0):
    np.random.seed(seed)
    _w = jnp.asarray

    def _rec_inputs():
        import jax
        import jax.numpy as jnp
        _rk = jax.random.key(seed)
        x = 7.22e-05 + 1 * jax.random.normal(jax.random.fold_in(_rk, 1), (128, 32, 512), jnp.float32)
        _lenS = 32 - jax.random.randint(jax.random.fold_in(_rk, 7), (128,), 0, max(1, 32 // 4) + 1, jnp.int32)
        _lenS2 = 257 - jax.random.randint(jax.random.fold_in(_rk, 8), (128,), 0, max(1, 257 // 4) + 1, jnp.int32)
        _ctx_768P = jax.random.normal(jax.random.fold_in(_rk, 11), (128, 16, 384), jnp.float32)
        _ctx_768c = jax.random.dirichlet(jax.random.fold_in(_rk, 511), 0.3 * jnp.ones((16,), jnp.float32), (128, 257))
        _ctx_768t = jnp.einsum('bsk,bkd->bsd', _ctx_768c, _ctx_768P)
        _ctx_768t = _ctx_768t * jax.lax.rsqrt(jnp.mean(jnp.square(_ctx_768t)) + 1e-12) * 0.953939
        ctx_768 = 2.09791e-05 + 1.00001 * (_ctx_768t + 0.3 * jax.random.normal(jax.random.fold_in(_rk, 611), (128, 257, 384), jnp.float32))
        return (x, ctx_768)
    x, ctx_768 = _rec_inputs()

    def _L0_xattn_setup():
        import jax, jax.numpy as jnp
        import numpy as np
        NUM_HEADS = 16
        key = jax.random.key(seed)
        ks = jax.random.split(key, 8)
        dim, cond_dim = (512, 384)
        B, N, condN = (4, 1024, 512)
        s = lambda k, shp, fan: jax.random.normal(k, shp, dtype=jnp.float32) * fan ** (-0.5)
        return {'x': jax.random.normal(ks[0], (B, N, dim), dtype=jnp.float32), 'cond': jax.random.normal(ks[1], (B, condN, cond_dim), dtype=jnp.float32), 'q_w': s(ks[2], (dim, dim), dim), 'q_b': jnp.zeros((dim,), jnp.float32), 'kv_w': s(ks[3], (cond_dim, 2 * dim), cond_dim), 'kv_b': jnp.zeros((2 * dim,), jnp.float32), 'proj_w': s(ks[4], (dim, dim), dim), 'proj_b': jnp.zeros((dim,), jnp.float32)}
    _L0_xattn_all = _L0_xattn_setup()
    _L0_xattn_in = {k: v for k, v in _L0_xattn_all.items() if k in ('q_w', 'q_b', 'kv_w', 'kv_b', 'proj_w', 'proj_b')}
    del _L0_xattn_all

    def _L0_attn_setup():
        import jax, jax.numpy as jnp
        import numpy as np
        B, L, D_IN, D_OUT, H = (4, 1024, 512, 512, 16)
        DH = D_OUT // H
        EPS = 1e-06

        def _rmsnorm(x, w):
            var = jnp.mean(jnp.square(x), axis=-1, keepdims=True)
            return x * jax.lax.rsqrt(var + EPS) * w
        key = jax.random.key(seed)
        ks = jax.random.split(key, 12)
        s_in = 1.0 / np.sqrt(D_IN)
        s_out = 1.0 / np.sqrt(D_OUT)
        return {'x': jax.random.normal(ks[0], (B, L, D_IN), jnp.float32), 'Wq': jax.random.normal(ks[1], (D_OUT, D_IN), jnp.float32) * s_in, 'Wk': jax.random.normal(ks[2], (D_OUT, D_IN), jnp.float32) * s_in, 'Wv': jax.random.normal(ks[3], (D_OUT, D_IN), jnp.float32) * s_in, 'Wg': jax.random.normal(ks[4], (D_OUT, D_IN), jnp.float32) * s_in, 'Wb': jax.random.normal(ks[5], (D_OUT, D_IN), jnp.float32) * s_in, 'Wa': jax.random.normal(ks[6], (H, D_IN), jnp.float32) * s_in, 'dt_bias': jnp.ones((H,), jnp.float32), 'A_log': jnp.log(jax.random.uniform(ks[7], (H,), jnp.float32, 0.001, 16.0)), 'norm_w': jnp.ones((DH,), jnp.float32), 'Wo': jax.random.normal(ks[8], (D_OUT, D_OUT), jnp.float32) * s_out, 'bo': jnp.zeros((D_OUT,), jnp.float32)}
    _L0_attn_all = _L0_attn_setup()
    _L0_attn_in = {k: v for k, v in _L0_attn_all.items() if k in ('Wq', 'Wk', 'Wv', 'Wg', 'Wb', 'Wa', 'dt_bias', 'A_log', 'norm_w', 'Wo', 'bo')}
    del _L0_attn_all

    def _L0_ffn_setup():
        import jax, jax.numpy as jnp
        import numpy as np
        NUM_EXPERTS = 8
        TOP_K = 2
        N_EMBD = 512
        B, T = (4, 1024)
        key = jax.random.key(seed)
        k_x, k_g, k_e = jax.random.split(key, 3)
        x = jax.random.normal(k_x, (B, T, N_EMBD), dtype=jnp.float32)
        scale = 1.0 / np.sqrt(N_EMBD)
        gate_w = jax.random.uniform(k_g, (NUM_EXPERTS, N_EMBD), dtype=jnp.float32, minval=-scale, maxval=scale)
        expert_w = jax.random.uniform(k_e, (NUM_EXPERTS, N_EMBD, N_EMBD), dtype=jnp.float32, minval=-scale, maxval=scale)
        return {'x': x, 'gate_w': gate_w, 'expert_w': expert_w}
    _L0_ffn_all = _L0_ffn_setup()
    _L0_ffn_in = {k: v for k, v in _L0_ffn_all.items() if k in ('gate_w', 'expert_w')}
    del _L0_ffn_all
    return {'x': x, 'ctx_768': ctx_768, 'L0_xattn_q_w': _L0_xattn_in['q_w'], 'L0_xattn_q_b': _L0_xattn_in['q_b'], 'L0_xattn_kv_w': _L0_xattn_in['kv_w'], 'L0_xattn_kv_b': _L0_xattn_in['kv_b'], 'L0_xattn_proj_w': _L0_xattn_in['proj_w'], 'L0_xattn_proj_b': _L0_xattn_in['proj_b'], 'L0_attn_Wq': _L0_attn_in['Wq'], 'L0_attn_Wk': _L0_attn_in['Wk'], 'L0_attn_Wv': _L0_attn_in['Wv'], 'L0_attn_Wg': _L0_attn_in['Wg'], 'L0_attn_Wb': _L0_attn_in['Wb'], 'L0_attn_Wa': _L0_attn_in['Wa'], 'L0_attn_dt_bias': _L0_attn_in['dt_bias'], 'L0_attn_A_log': _L0_attn_in['A_log'], 'L0_attn_norm_w': _L0_attn_in['norm_w'], 'L0_attn_Wo': _L0_attn_in['Wo'], 'L0_attn_bo': _L0_attn_in['bo'], 'L0_ffn_gate_w': _L0_ffn_in['gate_w'], 'L0_ffn_expert_w': _L0_ffn_in['expert_w']}

def reference(x, ctx_768, L0_xattn_q_w, L0_xattn_q_b, L0_xattn_kv_w, L0_xattn_kv_b, L0_xattn_proj_w, L0_xattn_proj_b, L0_attn_Wq, L0_attn_Wk, L0_attn_Wv, L0_attn_Wg, L0_attn_Wb, L0_attn_Wa, L0_attn_dt_bias, L0_attn_A_log, L0_attn_norm_w, L0_attn_Wo, L0_attn_bo, L0_ffn_gate_w, L0_ffn_expert_w):
    import jax
    import jax.numpy as jnp

    def _L0_xattn_ref(x, cond, q_w, q_b, kv_w, kv_b, proj_w, proj_b):
        import jax, jax.numpy as jnp
        import numpy as np
        NUM_HEADS = 16
        B, N, C = x.shape
        condN = cond.shape[1]
        H = NUM_HEADS
        hd = C // H
        scale = hd ** (-0.5)
        q = (x @ q_w + q_b).reshape(B, N, H, hd).transpose(0, 2, 1, 3)
        kv = (cond @ kv_w + kv_b).reshape(B, condN, 2, H, hd)
        k = kv[:, :, 0].transpose(0, 2, 1, 3)
        v = kv[:, :, 1].transpose(0, 2, 1, 3)
        attn = jnp.einsum('bhnd,bhmd->bhnm', q * scale, k)
        attn = jax.nn.softmax(attn, axis=-1)
        out = jnp.einsum('bhnm,bhmd->bhnd', attn, v)
        out = out.transpose(0, 2, 1, 3).reshape(B, N, C)
        return out @ proj_w + proj_b

    def _L0_attn_ref(x, Wq, Wk, Wv, Wg, Wb, Wa, dt_bias, A_log, norm_w, Wo, bo):
        import jax, jax.numpy as jnp
        import numpy as np
        B, L, D_IN, D_OUT, H = (4, 1024, 512, 512, 16)
        DH = D_OUT // H
        EPS = 1e-06

        def _rmsnorm(x, w):
            var = jnp.mean(jnp.square(x), axis=-1, keepdims=True)
            return x * jax.lax.rsqrt(var + EPS) * w
        b, l, _ = x.shape
        q = (x @ Wq.T).reshape(b, l, H, DH)
        k = (x @ Wk.T).reshape(b, l, H, DH)
        v = (x @ Wv.T).reshape(b, l, H, DH)
        gate = (x @ Wg.T).reshape(b, l, H, DH)
        beta = jax.nn.sigmoid(x @ Wb.T).reshape(b, l, H, DH)
        alpha = jnp.exp(-jnp.exp(A_log)[None, None, :] * jax.nn.softplus(x @ Wa.T + dt_bias))
        q = q / jnp.linalg.norm(q, axis=-1, keepdims=True) / np.sqrt(DH)
        k = k / jnp.linalg.norm(k, axis=-1, keepdims=True)

        def step(S, inp):
            k_t, q_t, v_t, beta_t, a_t = inp
            S = S * a_t[..., None, None]
            kv_mem = jnp.einsum('bhd,bhde->bhe', k_t, S)
            delta = (v_t - kv_mem) * beta_t
            S = S + k_t[..., :, None] * delta[..., None, :]
            y_t = jnp.einsum('bhd,bhde->bhe', q_t, S)
            return (S, y_t)
        tfirst = lambda a: jnp.moveaxis(a, 1, 0)
        S0 = jnp.zeros((b, H, DH, DH), x.dtype)
        _, ys = jax.lax.scan(step, S0, (tfirst(k), tfirst(q), tfirst(v), tfirst(beta), tfirst(alpha)))
        ys = jnp.moveaxis(ys, 0, 1)
        ctx = _rmsnorm(ys, norm_w) * jax.nn.silu(gate)
        ctx = ctx.reshape(b, l, D_OUT)
        return ctx @ Wo.T + bo

    def _L0_ffn_ref(x, gate_w, expert_w):
        import jax, jax.numpy as jnp
        import numpy as np
        NUM_EXPERTS = 8
        TOP_K = 2
        N_EMBD = 512
        B, T = (4, 1024)
        Bb, Tt, C = x.shape
        xf = x.reshape(Bb * Tt, C)
        logits = xf @ gate_w.T
        w, sel = jax.lax.top_k(logits, TOP_K)
        w = jax.nn.softmax(w.astype(jnp.float32), axis=1).astype(xf.dtype)
        n = xf.shape[0]
        w_full = jnp.zeros((n, NUM_EXPERTS), dtype=xf.dtype)
        w_full = w_full.at[jnp.arange(n)[:, None], sel].add(w)
        expert_out = jnp.einsum('nc,edc->ned', xf, expert_w)
        out = jnp.einsum('ne,ned->nd', w_full, expert_out)
        return out.reshape(Bb, Tt, C)
    x = x + _L0_xattn_ref(_layernorm(x, axis=-1), ctx_768, L0_xattn_q_w, L0_xattn_q_b, L0_xattn_kv_w, L0_xattn_kv_b, L0_xattn_proj_w, L0_xattn_proj_b)
    x = x + _L0_attn_ref(_layernorm(x, axis=-1), L0_attn_Wq, L0_attn_Wk, L0_attn_Wv, L0_attn_Wg, L0_attn_Wb, L0_attn_Wa, L0_attn_dt_bias, L0_attn_A_log, L0_attn_norm_w, L0_attn_Wo, L0_attn_bo)
    x = x + _L0_ffn_ref(_layernorm(x, axis=-1), L0_ffn_gate_w, L0_ffn_expert_w)
    return x

_drawn_inputs = setup_inputs


def setup_inputs(seed=0):
    import zlib

    import numpy as np

    out = dict(_drawn_inputs(seed))
    spreads = {'L0_xattn_q_b': (0.0, 0.1),
     'L0_xattn_kv_b': (0.0, 0.1),
     'L0_xattn_proj_b': (0.0, 0.1),
     'L0_attn_dt_bias': (1.0, 0.2),
     'L0_attn_norm_w': (1.0, 0.2),
     'L0_attn_bo': (0.0, 0.1)}
    factors = {}
    for name, (base, spread) in spreads.items():
        noise = np.random.default_rng([zlib.crc32(name.encode()), seed]).standard_normal(out[name].shape)
        drawn = base * np.exp(spread * noise) if base else spread * noise
        out[name] = jnp.asarray(drawn.astype(out[name].dtype))
    for name, factor in factors.items():
        out[name] = (out[name] * factor).astype(out[name].dtype)
    return out
```

```python
import concourse.bass as bass
import concourse.mybir as mybir
from concourse.alu_op_type import AluOpType as ALU
from contextlib import ExitStack

ACT = mybir.ActivationFunctionType
AX = mybir.AxisListType
F32 = mybir.dt.float32
F32R = mybir.dt.float32r
U32 = mybir.dt.uint32

B, N, D = 128, 32, 512
M, C = 257, 384
H, HD = 16, 32
E = 8
P = 128
BU = P // N
NU = B // BU
DC, CC = D // P, C // P
HG = H // 4
MU = BU * M
KEYS = (P, M - 1 - P)
PIECES = ((0, 344), (344, 342), (686, 342))
SCALE = HD ** -0.5
LN_EPS, RMS_EPS = 1e-5, 1e-6


class Ring:

    A = ["K00", "K01", "K02", "K03", "K10", "K11", "K12", "K13", "XT", "K20", "K21", "K22", "K23", "QT",
         "V00", "V01", "L0", "O0", "V10", "V11", "L1", "O1", "V20", "V21", "L2", "O2", "V30", "V31", "L3",
         "O3", "PR"]
    BOTH = ["K00", "K01", "K02", "K03", "X1T", "K10", "K11", "KK", "QQ", "K12", "K13", "XT", "K20", "K21",
            "V2", "BT", "GT", "AL", "K22", "K23", "QT", "D0", "D1", "D2", "D3"] + A[14:]
    B = ["X1T", "KK", "QQ", "V2", "BT", "GT", "AL", "D0", "D1", "D2", "D3"]

    def __init__(self, full, free):
        self.full, self.free = full, free
        assert len(self.BOTH) % 2 == 0

    def use(self, name, u):
        if isinstance(u, int) and u == 0:
            n = self.A.index(name)
            return n % 2, n // 2
        if isinstance(u, int) and u == NU:
            n = len(self.A) + (NU - 1) * len(self.BOTH) + self.B.index(name)
            return n % 2, n // 2
        n = len(self.A) + self.BOTH.index(name)
        return n % 2, (u - 1) * (len(self.BOTH) // 2) + n // 2

    def claim(self, pe, name, u):
        bank, before = self.use(name, u)
        if not (isinstance(before, int) and before == 0):
            pe.wait_ge(self.free[bank], before)
        return bank

    def wait_full(self, eng, name, u):
        bank, before = self.use(name, u)
        eng.wait_ge(self.full[bank], before + 1)
        return bank

    def wait_read(self, eng, name, u):
        bank, before = self.use(name, u)
        eng.wait_ge(self.free[bank], before + 1)


def wait_apart(eng, sem, count):
    eng.wait_ge(sem, 1)
    eng.wait_ge(sem, count)


class Own:

    def __init__(self, eng, sem, carrier=None):
        self.eng, self.sem, self.carrier, self.base, self.n = eng, sem, carrier, 0, 0

    def did(self, ins):
        ins.then_inc(self.sem, 1)
        self.n += 1
        return self.base + self.n

    def wait(self, count):
        self.eng.wait_ge(self.sem, count)

    def then(self, ins):
        self.wait(self.did(ins))

    def then_apart(self, ins):
        self.then(ins)
        self.did(self.carrier())

    def turn(self, start, number, per_turn):
        self.base, self.n = start + number * per_turn, 0


def split_exactly(eng, own, high, low, whole):
    own.then(eng.tensor_copy(high, whole))
    return eng.tensor_tensor(low, whole, high.bitcast(F32), ALU.subtract)


def products(pe, out, terms):
    for i, (lhs_t, rhs) in enumerate(terms):
        last = pe.matmul(out, lhs_t, rhs, start=(i == 0), stop=(i == len(terms) - 1))
    return last


def split_terms(lhs_t, rhs):
    (lh, ll), (rh, rl) = lhs_t, rhs
    return [(lh, rh), (lh, rl), (ll, rh)]


def build(nc, x, cond_t, cond_last_t, q_w, q_b, kv_w, kv_b, proj_w, proj_b, attn_w_t, wa_t, dt_bias, a_log,
          norm_w, wo_t, bo, gate_t, expert_t, out):
    v_last_d = nc.dram_tensor("v_last", [B, D], F32).ap()
    x1_d = nc.dram_tensor("x1_rows", [B, N, D], F32).ap()
    vgb_d = nc.dram_tensor("vgb_rows", [B, N, 3 * D], F32).ap()
    small_d = nc.dram_tensor("small_rows", [B, N, 3 * H], F32).ap()
    gram_d = nc.dram_tensor("gram_rows", [B, 2, N, D], F32).ap()
    with ExitStack() as both:
        ident = both.enter_context(nc.sbuf_tensor("ident", [P, P], F32))
        cross_pass(nc, ident, x, cond_t, cond_last_t, q_w, q_b, kv_w, kv_b, proj_w, proj_b, attn_w_t, wa_t,
                   v_last_d, x1_d, vgb_d, small_d, gram_d)
        time_pass(nc, ident, x1_d, vgb_d, small_d, gram_d, dt_bias, a_log, norm_w, wo_t, bo, gate_t,
                  expert_t, out)


def cross_pass(nc, ident, x, cond_t, cond_last_t, q_w, q_b, kv_w, kv_b, proj_w, proj_b, attn_w_t, wa_t,
               v_last_d, x1_d, vgb_d, small_d, gram_d):
    with ExitStack() as ctx:
        def sb(name, shape, dt=F32):
            return ctx.enter_context(nc.sbuf_tensor(name, shape, dt))

        def sem(name):
            return ctx.enter_context(nc.semaphore(name))

        wq = sb("wq", [P, DC, D])
        wkv_high = sb("wkv_high", [P, CC, 2 * D], F32R)
        wkv_low = sb("wkv_low", [P, CC, 2 * D], F32R)
        wproj = sb("wproj", [P, HG, D])
        wattn = sb("wattn", [P, 5, DC, D])
        wa = sb("wa", [P, DC, H])
        qb = sb("qb", [P, HG])
        kvb = sb("kvb", [P, 2 * HG])
        projb = sb("projb", [P, D])
        head_of = sb("head_of", [P, HG, H])

        cond = sb("cond", [P, CC, MU])
        cond_high = sb("cond_high", [P, CC, MU], F32R)
        cond_low = sb("cond_low", [P, CC, MU], F32R)
        x_in = sb("x_in", [P, D])
        x_res = sb("x_res", [P, D])
        xn = sb("xn", [P, D])
        xn_t = sb("xn_t", [P, DC, P])
        q_s = sb("q_s", [P, HG, P])
        q_diag = sb("q_diag", [P, HG * BU, P])
        k_t = sb("k_t", [P, HG, MU])
        v_s = sb("v_s", [P, 2, D])
        v_last = sb("v_last_s", [HG, BU, P])
        prob = sb("prob", [P, HG, M])
        prob_t = sb("prob_t", [P, 2, HG * P])
        prob_last_t = sb("prob_last_t", [HG, HG, P])
        neg_max = sb("neg_max", [P, HG])
        sums = sb("sums", [P, HG])
        inv_sums = sb("inv_sums", [P, HG])
        att_t = sb("att_t", [P, HG, P])
        x1 = sb("x1", [P, D])
        x1n = sb("x1n", [P, D])
        x1n_t = sb("x1n_t", [P, DC, P])
        kq = sb("kq", [P, HG * BU, 2 * N])
        k_diag = sb("k_diag", [P, HG * BU, P])
        squares = sb("squares", [P, 2, D])
        vgb = sb("vgb", [P, 3, D])
        small = sb("small", [P, 3 * H])
        gram = sb("gram", [2 * N, 2, D])
        stats = sb("stats", [P, 6])
        mean_var = sb("mean_var", [P, 2])
        var_eps = sb("var_eps", [P, 2])
        rstd = sb("rstd", [P, 2])
        minus_half = sb("minus_half", [P, 1])
        tick, tick_v = sb("tick", [P, 1]), sb("tick_v", [P, 1])

        with ExitStack() as pre:
            wkv = k_t[:].rearrange("p g n -> p (g n)")[:, 0:CC * 2 * D].rearrange("p (c n) -> p c n", c=CC)
            cond_last = cond[:, :, 0:B]
            v_last_all = x1[0:B, :]
            bank = pre.enter_context(nc.psum_tensor("v_last_bank", [B, D], F32))
            loaded = pre.enter_context(nc.semaphore("weights_loaded"))
            kv_loaded = pre.enter_context(nc.semaphore("kv_loaded"))
            pool_own = pre.enter_context(nc.semaphore("setup_pool_steps"))
            dve_own = pre.enter_context(nc.semaphore("setup_vector_steps"))
            v_last_ready = pre.enter_context(nc.semaphore("v_last_ready"))
            v_last_moved = pre.enter_context(nc.semaphore("v_last_moved"))
            v_last_stored = pre.enter_context(nc.semaphore("v_last_stored"))
            block = pre.enter_context(nc.Block())

            @block.sync
            def _(sp):
                sp.dma_start(wkv, kv_w.rearrange("(c p) n -> p c n", p=P)).then_inc(kv_loaded, 16)
                sp.dma_start(cond_last, cond_last_t.rearrange("(c p) n -> p c n", p=P)).then_inc(kv_loaded, 16)
                loads = [(wq[:], q_w.rearrange("(c p) n -> p c n", p=P)),
                         (wproj[:], proj_w.rearrange("(c p) n -> p c n", p=P)),
                         (wa[:], wa_t.rearrange("(c p) n -> p c n", p=P)),
                         (qb[:], q_b),
                         (kvb[:], kv_b),
                         (projb[:], proj_b.rearrange("(a n) -> a n", a=1).to_broadcast([P, D]))]
                loads += [(wattn[:, i], attn_w_t[i].rearrange("(c p) n -> p c n", p=P)) for i in range(5)]
                for dst, src in loads:
                    sp.dma_start(dst, src).then_inc(loaded, 16)
                sp.wait_ge(v_last_moved, 1)
                sp.dma_start(v_last_d, v_last_all).then_inc(v_last_stored, 16)
                sp.wait_ge(v_last_stored, 16)
                sp.wait_ge(loaded, 16 * len(loads))

            @block.gpsimd
            def _(pool):
                own = Own(pool, pool_own)
                own.did(pool.memset(minus_half[:], -0.5))
                own.did(pool.memset(q_diag[:], 0.0))
                own.did(pool.memset(k_diag[:], 0.0))
                own.did(pool.memset(head_of[:], 1.0))
                own.then(pool.memset(ident[:], 0.0))
                own.did(pool.affine_select(out=ident[:], in_=ident[:], compare_op=ALU.not_equal, fill=1.0, base=0,
                                           pattern=[[-1, P]], channel_multiplier=1))
                own.then(pool.affine_select(out=head_of[:], in_=head_of[:], compare_op=ALU.is_ge, fill=0.0,
                                            base=0, pattern=[[P, HG], [-HD, H]], channel_multiplier=1))
                own.then(pool.affine_select(out=head_of[:], in_=head_of[:], compare_op=ALU.is_ge, fill=0.0,
                                            base=HD - 1, pattern=[[-P, HG], [HD, H]], channel_multiplier=-1))

            @block.vector
            def _(dve):
                own = Own(dve, dve_own)
                dve.wait_ge(kv_loaded, 32)
                own.then(split_exactly(dve, own, wkv_high[:], wkv_low[:], wkv))
                dve.wait_ge(v_last_ready, 1)
                dve.tensor_copy(v_last_all, bank[:]).then_inc(v_last_moved, 1)

            @block.tensor
            def _(pe):
                pe.wait_ge(kv_loaded, 32)
                products(pe, bank[:], [(cond_last[:, c, :], wkv[:, c, D:]) for c in range(CC)]).then_inc(v_last_ready, 1)

        ring_bank = [ctx.enter_context(nc.psum_tensor(f"ring{i}", [P, D], F32)) for i in range(2)]
        score = ctx.enter_context(nc.psum_tensor("score", [P, HG, D], F32))
        turned = [ctx.enter_context(nc.psum_tensor(f"turned{i}", [P, HG * P], F32)) for i in range(2)]

        ring = Ring([sem("ring0_full"), sem("ring1_full")], [sem("ring0_free"), sem("ring1_free")])
        cond_loaded, x_loaded, v_last_loaded = sem("cond_loaded"), sem("x_loaded"), sem("v_last_loaded")
        x_used = sem("x_used")
        split_done = sem("split_done")
        var_ready, rstd_ready = sem("var_ready"), sem("rstd_ready")
        xn_ready, x1n_ready = sem("xn_ready"), sem("x1n_ready")
        q_diag_ready = sem("q_diag_ready")
        score_ready, neg_max_ready = sem("score_ready"), sem("neg_max_ready")
        exp_done, prob_ready = sem("exp_done"), sem("prob_ready")
        turned_ready, prob_t0_ready, prob_t1_ready = sem("turned_ready"), sem("prob_t0_ready"), sem("prob_t1_ready")
        kq_ready, k_diag_ready = sem("kq_ready"), sem("k_diag_ready")
        x1_stored, vgb_stored, small_stored = sem("x1_stored"), sem("vgb_stored"), sem("small_stored")
        gram_stored = [sem("gram0_stored"), sem("gram1_stored")]
        dve_steps, pool_steps = sem("vector_steps"), sem("pool_steps")

        block = ctx.enter_context(nc.Block())
        rows_x = x.rearrange("b t n -> (b t) n")
        rows_x1 = x1_d.rearrange("b t n -> (b t) n")
        rows_vgb = vgb_d.rearrange("b t n -> (b t) n")
        rows_small = small_d.rearrange("b t n -> (b t) n")
        rows_gram = gram_d.rearrange("b w t n -> (b w t) n")
        cond_v = cond_t.rearrange("(c p) n -> p c n", p=P)

        @block.sync
        def _(sp):
            def load_cond(u):
                if not (isinstance(u, int) and u == 0):
                    sp.wait_ge(split_done, u * BU)
                sp.dma_start(cond[:], cond_v[:, :, bass.ds(u * MU, MU)]).then_inc(cond_loaded, 16)

            def load_x(u):
                if not (isinstance(u, int) and u == 0):
                    sp.wait_ge(x_used, u)
                sp.dma_start(x_in[:], rows_x[bass.ds(u * P, P), :]).then_inc(x_loaded, 16)

            def load_v_last(u):
                if not (isinstance(u, int) and u == 0):
                    ring.wait_full(sp, "PR", u - 1)
                sp.dma_start(v_last[:], v_last_d[bass.ds(u * BU, BU), :].rearrange("b (g j) -> g b j", g=HG))\
                    .then_inc(v_last_loaded, 16)

            def store_results(u):
                ring.wait_read(sp, "GT", u)
                sp.dma_start(rows_vgb[bass.ds((u - 1) * P, P), :], vgb[:].rearrange("p a n -> p (a n)"))\
                    .then_inc(vgb_stored, 16)
                ring.wait_read(sp, "AL", u)
                sp.dma_start(rows_small[bass.ds((u - 1) * P, P), :], small[:]).then_inc(small_stored, 16)
                for b in range(BU):
                    ring.wait_read(sp, f"D{b}", u)
                    sp.dma_start(rows_gram[bass.ds(((u - 1) * BU + b) * 2 * N, 2 * N), :], gram[:, b % 2, :])\
                        .then_inc(gram_stored[b % 2], 16)

            def store_x1(u):
                ring.wait_read(sp, "PR", u - 1)
                sp.dma_start(rows_x1[bass.ds((u - 1) * P, P), :], x1[:]).then_inc(x1_stored, 16)

            load_cond(0)
            load_x(0)
            load_v_last(0)
            load_cond(1)
            load_x(1)
            with sp.Fori(1, NU - 1) as u:
                store_x1(u)
                load_v_last(u)
                load_cond(u + 1)
                load_x(u + 1)
                store_results(u)
            store_x1(NU - 1)
            load_v_last(NU - 1)
            store_results(NU - 1)
            store_x1(NU)
            store_results(NU)
            for done, n in ((x1_stored, NU), (vgb_stored, NU), (small_stored, NU),
                            (gram_stored[0], 2 * NU), (gram_stored[1], 2 * NU)):
                sp.wait_ge(done, 16 * n)

        @block.gpsimd
        def _(pool):
            own = Own(pool, pool_steps, lambda: pool.tensor_tensor(tick[:], minus_half[:], minus_half[:], ALU.add))

            def split(u):
                pool.wait_ge(cond_loaded, 16 * u + 16)
                for b in range(BU):
                    if not (isinstance(u, int) and u == 0):
                        ring.wait_full(pool, f"V{b}1", u - 1)
                        own.did(own.carrier())
                    cols = slice(b * M, (b + 1) * M)
                    split_exactly(pool, own, cond_high[:, :, cols], cond_low[:, :, cols], cond[:, :, cols])\
                        .then_inc(split_done, 1)

            def norm_power(i, count):
                pool.wait_ge(var_ready, count)
                pool.tensor_tensor(rstd[:, i:i + 1], var_eps[:, i:i + 1], minus_half[:], ALU.pow).then_inc(rstd_ready, 1)

            split(0)
            norm_power(0, 1)
            split(1)
            norm_power(1, 2)
            with pool.Fori(1, NU - 1) as u:
                own.turn(3 * BU, u - 1, 2 * BU)
                norm_power(0, 2 * u + 1)
                split(u + 1)
                assert own.n == 2 * BU
                norm_power(1, 2 * u + 2)
            norm_power(0, 2 * (NU - 1) + 1)
            norm_power(1, 2 * (NU - 1) + 2)

        @block.scalar
        def _(act):
            def move(name, u, dst, **how):
                bank = ring.wait_full(act, name, u)
                act.activation(dst, ring_bank[bank][:], ACT.Copy, **how).then_inc(ring.free[bank], 1)

            def move_keys(u, piece, group):
                bank = ring.wait_full(act, f"K{piece}{group}", u)
                at, n = PIECES[piece]
                act.activation(k_t[:, group, at:at + n], ring_bank[bank][:, 0:n], ACT.Identity,
                               bias=kvb[:, group:group + 1]).then_inc(ring.free[bank], 1)

            def move_kq(u, i, name):
                bank = ring.wait_full(act, name, u)
                act.activation(kq[:, :, i * N:i * N + N], ring_bank[bank][:].rearrange("p (g t) -> p g t", t=N),
                               ACT.Copy).then_inc(kq_ready, 1)
                act.activation(squares[:, i, :], ring_bank[bank][:], ACT.Square).then_inc(ring.free[bank], 1)

            def turn(u, first=False, last=False):
                a, b_ = not last, not first
                if a:
                    for g in range(4):
                        move_keys(u, 0, g)
                if b_:
                    move("X1T", u, x1n_t[:].rearrange("p c t -> p (c t)"))
                if a:
                    move_keys(u, 1, 0)
                    move_keys(u, 1, 1)
                if b_:
                    move_kq(u, 0, "KK")
                    move_kq(u, 1, "QQ")
                    act.wait_ge(kq_ready, 2 * u)
                    for h in range(4):
                        rows = slice(HD * h, HD * h + HD)
                        ins = act.activation(k_diag[rows, :, HD * h:HD * h + HD], kq[rows, :, 0:N], ACT.Copy)
                    ins.then_inc(k_diag_ready, 1)
                if a:
                    move_keys(u, 1, 2)
                    move_keys(u, 1, 3)
                    move("XT", u, xn_t[:].rearrange("p c t -> p (c t)"))
                    move_keys(u, 2, 0)
                    move_keys(u, 2, 1)
                if b_:
                    wait_stored(act, vgb_stored, u)
                    move("V2", u, vgb[:, 0, :])
                    move("BT", u, vgb[:, 2, :])
                    move("GT", u, vgb[:, 1, :])
                    wait_stored(act, small_stored, u)
                    bank = ring.wait_full(act, "AL", u)
                    act.activation(small[:], ring_bank[bank][:, 0:3 * H], ACT.Copy).then_inc(ring.free[bank], 1)
                if a:
                    move_keys(u, 2, 2)
                    move_keys(u, 2, 3)
                if b_:
                    for b in range(BU):
                        if not (isinstance(u, int) and u == 1 and b < 2):
                            act.wait_ge(gram_stored[b % 2], ((u - 1) * 2 + b // 2) * 16)
                        bank = ring.wait_full(act, f"D{b}", u)
                        act.activation(gram[:, b % 2, :], ring_bank[bank][0:2 * N, :], ACT.Copy)\
                            .then_inc(ring.free[bank], 1)
                if a:
                    for b in range(BU):
                        n = u * BU + b
                        act.wait_ge(neg_max_ready, n + 1)
                        for g in range(HG):
                            act.activation(prob[:, g, :], score[:, g, 0:M], ACT.Exp, bias=neg_max[:, g:g + 1],
                                           accum_out=sums[:, g:g + 1]).then_inc(exp_done, 1)
                        move(f"V{b}0", u, v_s[:, 0, :])
                        move(f"V{b}1", u, v_s[:, 1, :])
                        act.wait_ge(turned_ready, n + 1)
                        act.activation(prob_t[:, 0, :], turned[0][:], ACT.Copy).then_inc(prob_t0_ready, 1)

            def wait_stored(eng, stored, u):
                if not (isinstance(u, int) and u == 1):
                    eng.wait_ge(stored, (u - 1) * 16)

            turn(0, first=True)
            turn(1)
            with act.Fori(2, NU) as u:
                turn(u)
            turn(NU, last=True)

        @block.vector
        def _(dve):
            own = Own(dve, dve_steps, lambda: dve.tensor_copy(tick_v[:], minus_half[:]))

            def norm(rows, i, count, dst):
                own.then_apart(dve.bn_stats(stats[:], rows))
                own.then(dve.bn_aggr(mean_var[:], stats[:]))
                dve.tensor_scalar(var_eps[:, i:i + 1], mean_var[:, 1:2], LN_EPS, None, ALU.add).then_inc(var_ready, 1)
                dve.wait_ge(rstd_ready, count)
                return dve.tensor_scalar(dst, rows, mean_var[:, 0:1], rstd[:, i:i + 1], ALU.subtract, ALU.mult)

            def turn(u):
                n0 = u * BU
                first = isinstance(u, int) and u == 0
                dve.wait_ge(x_loaded, 16 * u + 16)
                norm(x_in[:], 0, 2 * u + 1, xn[:]).then_inc(xn_ready, 1)
                dve.tensor_tensor(x_res[:], x_in[:], projb[:], ALU.add).then_inc(x_used, 1)
                bank = ring.wait_full(dve, "QT", u)
                own.then(dve.tensor_tensor(q_s[:], ring_bank[bank][:].rearrange("p (g t) -> p g t", g=HG),
                                           qb[:].unsqueeze(2).to_broadcast([P, HG, P]), ALU.add))
                for h in range(4):
                    rows = slice(HD * h, HD * h + HD)
                    src = q_s[rows].rearrange("p g (b t) -> p (g b) t", t=N)
                    last = dve.tensor_scalar(q_diag[rows, :, HD * h:HD * h + HD], src, SCALE, None, ALU.mult)
                    if h == 0:
                        last.then_inc(ring.free[bank], 1)
                last.then_inc(q_diag_ready, 1)

                def maximum(b):
                    dve.wait_ge(score_ready, n0 + b + 1)
                    dve.tensor_reduce(neg_max[:], score[:, :, 0:M], AX.X, ALU.max, negate=True)\
                        .then_inc(neg_max_ready, 1)

                def normalise(b):
                    dve.wait_ge(exp_done, (n0 + b + 1) * HG)
                    own.then(dve.reciprocal(inv_sums[:], sums[:]))
                    for g in range(HG):
                        last = dve.tensor_scalar(prob[:, g, :], prob[:, g, :], inv_sums[:, g:g + 1], None, ALU.mult)
                    last.then_inc(prob_ready, 1)

                def move_turned(b):
                    dve.wait_ge(turned_ready, n0 + b + 1)
                    dve.tensor_copy(prob_t[:, 1, :], turned[1][:]).then_inc(prob_t1_ready, 1)
                    bank = ring.wait_full(dve, f"L{b}", u)
                    dve.tensor_tensor(prob_last_t[:],
                                      ring_bank[bank][0:HG, 0:P].unsqueeze(1).to_broadcast([HG, HG, P]),
                                      ident[0:HG, 0:HG].unsqueeze(2).to_broadcast([HG, HG, P]), ALU.mult)\
                        .then_inc(ring.free[bank], 1)

                def move_attended(b):
                    bank = ring.wait_full(dve, f"O{b}", u)
                    for h in range(4):
                        rows = slice(HD * h, HD * h + HD)
                        src = ring_bank[bank][rows, :].rearrange("p (g t) -> p g t", g=HG)[:, :, HD * h:HD * h + HD]
                        last = dve.tensor_tensor(att_t[rows, :, b * N:b * N + N], src,
                                                 kvb[rows, HG:].unsqueeze(2).to_broadcast([HD, HG, N]), ALU.add)
                    last.then_inc(ring.free[bank], 1)

                maximum(0)
                normalise(0)
                move_turned(0)
                for b in range(1, BU):
                    maximum(b)
                    move_attended(b - 1)
                    normalise(b)
                    move_turned(b)
                move_attended(BU - 1)
                bank = ring.wait_full(dve, "PR", u)
                if not first:
                    dve.wait_ge(x1_stored, 16 * u)
                dve.tensor_tensor(x1[:], ring_bank[bank][:], x_res[:], ALU.add).then_inc(ring.free[bank], 1)
                ring.wait_read(dve, "PR", u)
                norm(x1[:], 1, 2 * u + 2, x1n[:]).then_inc(x1n_ready, 1)

            turn(0)
            per_turn = own.n
            with dve.Fori(1, NU) as u:
                own.turn(per_turn, u - 1, per_turn)
                turn(u)
                assert own.n == per_turn

        @block.tensor
        def _(pe):
            def bank_of(name, u):
                bank = ring.claim(pe, name, u)
                return ring_bank[bank], ring.full[bank]

            def keys(u, piece, group):
                at, n = PIECES[piece]
                if group == 0:
                    pe.wait_ge(split_done, u * BU + piece + 2)
                bank, full = bank_of(f"K{piece}{group}", u)
                terms = []
                for c in range(CC):
                    w = slice(group * P, group * P + P)
                    terms += split_terms((wkv_high[:, c, w], wkv_low[:, c, w]),
                                         (cond_high[:, c, at:at + n], cond_low[:, c, at:at + n]))
                products(pe, bank[:, 0:n], terms).then_inc(full, 1)

            def values(u, b, j):
                bank, full = bank_of(f"V{b}{j}", u)
                terms = []
                for c in range(CC):
                    k = slice(b * M + j * P, b * M + j * P + P)
                    terms += split_terms((cond_high[:, c, k], cond_low[:, c, k]),
                                         (wkv_high[:, c, D:], wkv_low[:, c, D:]))
                products(pe, bank[:], terms).then_inc(full, 1)

            def turn_rows(name, u, rows):
                bank, full = bank_of(name, u)
                for c in range(DC):
                    last = pe.transpose(bank[:, c * P:c * P + P], rows[:, c * P:c * P + P], ident[:])
                last.then_inc(full, 1)

            def by_channel(name, u, weights, rows_t):
                bank, full = bank_of(name, u)
                for g in range(HG):
                    w = slice(g * P, g * P + P)
                    last = products(pe, bank[:, w], [(weights[:, c, w], rows_t[:, c, :]) for c in range(DC)])
                last.then_inc(full, 1)

            def by_token(name, u, rows_t, weights):
                bank, full = bank_of(name, u)
                products(pe, bank[:], [(rows_t[:, c, :], weights[:, c, :]) for c in range(DC)]).then_inc(full, 1)

            def small_columns(u):
                bank, full = bank_of("AL", u)
                products(pe, bank[:, 0:H], [(x1n_t[:, c, :], wa[:, c, :]) for c in range(DC)])
                ring.wait_read(pe, "QQ", u)
                for i in range(2):
                    last = products(pe, bank[:, H + H * i:2 * H + H * i],
                                    [(squares[:, i, g * P:g * P + P], head_of[:, g, :]) for g in range(HG)])
                last.then_inc(full, 1)

            def scores(u, b):
                n = u * BU + b
                if not (isinstance(n, int) and n == 0):
                    pe.wait_ge(exp_done, n * HG)
                for g in range(HG):
                    last = pe.matmul(score[:, g, 0:M], q_diag[:, g * BU + b, :], k_t[:, g, b * M:b * M + M],
                                     start=True, stop=True)
                last.then_inc(score_ready, 1)

            def turn_probabilities(u, b):
                n = u * BU + b
                pe.wait_ge(prob_ready, n + 1)
                for j in range(2):
                    for g in range(HG):
                        last = pe.transpose(turned[j][:, g * P:g * P + P], prob[:, g, j * P:j * P + P], ident[:])
                last.then_inc(turned_ready, 1)
                bank, full = bank_of(f"L{b}", u)
                pe.matmul(bank[0:HG, 0:P], prob[:, :, M - 1], ident[:], start=True, stop=True).then_inc(full, 1)

            def attend(u, b):
                n = u * BU + b
                pe.wait_ge(prob_t0_ready, n + 1)
                pe.wait_ge(prob_t1_ready, n + 1)
                ring.wait_read(pe, f"L{b}", u)
                ring.wait_read(pe, f"V{b}1", u)
                if b == 0:
                    pe.wait_ge(v_last_loaded, 16 * u + 16)
                bank, full = bank_of(f"O{b}", u)
                for g in range(HG):
                    w = slice(g * P, g * P + P)
                    last = products(pe, bank[:, w], [(v_s[:, 0, w], prob_t[:, 0, w]), (v_s[:, 1, w], prob_t[:, 1, w]),
                                                     (v_last[:, b, :], prob_last_t[:, g, :])])
                last.then_inc(full, 1)

            def turn(u, first=False, last=False):
                a, b_ = not last, not first
                if a:
                    for g in range(4):
                        keys(u, 0, g)
                if b_:
                    pe.wait_ge(x1n_ready, u)
                    turn_rows("X1T", u, x1n)
                if a:
                    keys(u, 1, 0)
                    keys(u, 1, 1)
                if b_:
                    ring.wait_read(pe, "X1T", u)
                    by_channel("KK", u, wattn[:, 1], x1n_t)
                    by_channel("QQ", u, wattn[:, 0], x1n_t)
                if a:
                    keys(u, 1, 2)
                    keys(u, 1, 3)
                    pe.wait_ge(xn_ready, u + 1)
                    turn_rows("XT", u, xn)
                    keys(u, 2, 0)
                    keys(u, 2, 1)
                if b_:
                    by_token("V2", u, x1n_t, wattn[:, 2])
                    by_token("BT", u, x1n_t, wattn[:, 4])
                    by_token("GT", u, x1n_t, wattn[:, 3])
                    small_columns(u)
                if a:
                    keys(u, 2, 2)
                    keys(u, 2, 3)
                    ring.wait_read(pe, "XT", u)
                    by_channel("QT", u, wq, xn_t)
                if b_:
                    pe.wait_ge(k_diag_ready, u)
                    for b in range(BU):
                        bank, full = bank_of(f"D{b}", u)
                        for g in range(HG):
                            i = g * BU + b
                            last_mm = pe.matmul(bank[0:2 * N, g * P:g * P + P], kq[:, i, :], k_diag[:, i, :],
                                                start=True, stop=True)
                        last_mm.then_inc(full, 1)
                if a:
                    ring.wait_read(pe, "K23", u)
                    pe.wait_ge(q_diag_ready, u + 1)
                    scores(u, 0)
                    values(u, 0, 0)
                    values(u, 0, 1)
                    turn_probabilities(u, 0)
                    for b in range(1, BU):
                        scores(u, b)
                        attend(u, b - 1)
                        values(u, b, 0)
                        values(u, b, 1)
                        turn_probabilities(u, b)
                    attend(u, BU - 1)
                    ring.wait_read(pe, "O3", u)
                    bank, full = bank_of("PR", u)
                    products(pe, bank[:], [(att_t[:, g, :], wproj[:, g, :]) for g in range(HG)]).then_inc(full, 1)

            turn(0, first=True)
            with pe.Fori(1, NU) as u:
                turn(u)
            turn(NU, last=True)


def time_pass(nc, ident, x1_d, vgb_d, small_d, gram_d, dt_bias, a_log, norm_w, wo_t, bo, gate_t, expert_t, out):
    with ExitStack() as ctx:
        def sb(name, shape, dt=F32):
            return ctx.enter_context(nc.sbuf_tensor(name, shape, dt))

        def sem(name):
            return ctx.enter_context(nc.semaphore(name))

        experts = sb("experts", [P, E, DC, D])
        wo = sb("wo", [P, DC, D])
        gate = sb("gate", [P, DC, E])
        normw = sb("normw", [B, HD])
        bo_s = sb("bo_s", [B, D])
        column = sb("column", [B, E])
        ones = sb("ones", [B, H])
        half_off = sb("half_off", [B, H])
        tick = sb("tick2", [B, 1])
        deltas = sb("deltas", [B, H, HD, N])
        decay = sb("decay", [B, H, N])
        alpha = sb("alpha", [B, N, H])
        inv_norm = sb("inv_norm", [B, N, 2 * H])

        with ExitStack() as pre:
            small = pre.enter_context(nc.sbuf_tensor("small_all", [B, N, 3 * H], F32))
            z = pre.enter_context(nc.sbuf_tensor("z", [B, N, H], F32))
            minus_abs = pre.enter_context(nc.sbuf_tensor("minus_abs", [B, N, H], F32))
            log_part = pre.enter_context(nc.sbuf_tensor("log_part", [B, N, H], F32))
            dtb = pre.enter_context(nc.sbuf_tensor("dtb", [B, H], F32))
            alog = pre.enter_context(nc.sbuf_tensor("alog", [B, H], F32))
            rate = pre.enter_context(nc.sbuf_tensor("rate", [B, H], F32))
            loaded = pre.enter_context(nc.semaphore("small_loaded"))
            weights = pre.enter_context(nc.semaphore("pass2_weights_loaded"))
            v_steps = pre.enter_context(nc.semaphore("prepare_vector_steps"))
            a_steps = pre.enter_context(nc.semaphore("prepare_scalar_steps"))
            block = pre.enter_context(nc.Block())

            def over_time(row):
                return row.unsqueeze(1).to_broadcast([B, N, H])

            @block.sync
            def _(sp):
                sp.dma_start(small[:], small_d).then_inc(loaded, 16)
                sp.dma_start(dtb[:], dt_bias.rearrange("(a n) -> a n", a=1).to_broadcast([B, H])).then_inc(loaded, 16)
                sp.dma_start(alog[:], a_log.rearrange("(a n) -> a n", a=1).to_broadcast([B, H])).then_inc(loaded, 16)
                loads = [(wo[:], wo_t.rearrange("(c p) n -> p c n", p=P)),
                         (gate[:], gate_t.rearrange("(c p) n -> p c n", p=P)),
                         (normw[:], norm_w.rearrange("(a n) -> a n", a=1).to_broadcast([B, HD])),
                         (bo_s[:], bo.rearrange("(a n) -> a n", a=1).to_broadcast([B, D]))]
                loads += [(experts[:, e], expert_t[e].rearrange("(c p) n -> p c n", p=P)) for e in range(E)]
                for dst, src in loads:
                    sp.dma_start(dst, src).then_inc(weights, 16)
                sp.wait_ge(weights, 16 * len(loads))

            @block.gpsimd
            def _(pool):
                pool.memset(deltas[:], 0.0)
                pool.memset(decay[:], 0.0)
                pool.memset(ones[:], 1.0)
                pool.memset(half_off[:], -0.5)
                for e in range(E):
                    pool.memset(column[:, e:e + 1], float(e))

            @block.vector
            def _(dve):
                dve.wait_ge(loaded, 48)
                dve.tensor_tensor(z[:], small[:, :, 0:H], over_time(dtb[:]), ALU.add).then_inc(v_steps, 1)
                dve.wait_ge(v_steps, 1)
                dve.scalar_tensor_tensor(minus_abs[:], z[:], -1.0, z[:], ALU.mult, ALU.min).then_inc(v_steps, 1)
                dve.wait_ge(a_steps, 3)
                dve.scalar_tensor_tensor(z[:], z[:], 0.0, log_part[:], ALU.max, ALU.add).then_inc(v_steps, 1)
                dve.wait_ge(v_steps, 3)
                dve.tensor_tensor(z[:], z[:], over_time(rate[:]), ALU.mult).then_inc(v_steps, 1)
                dve.wait_ge(a_steps, 5)
                dve.reciprocal(inv_norm[:], small[:, :, H:3 * H]).then_inc(v_steps, 1)
                dve.wait_ge(v_steps, 5)
                dve.tensor_scalar(inv_norm[:, :, H:2 * H], inv_norm[:, :, H:2 * H], SCALE, None, ALU.mult)

            @block.scalar
            def _(act):
                act.wait_ge(v_steps, 2)
                act.activation(minus_abs[:], minus_abs[:], ACT.Exp).then_inc(a_steps, 1)
                act.activation(rate[:], alog[:], ACT.Exp).then_inc(a_steps, 1)
                act.wait_ge(a_steps, 1)
                act.activation(log_part[:], minus_abs[:], ACT.Ln, bias=1.0).then_inc(a_steps, 1)
                act.wait_ge(v_steps, 4)
                act.activation(alpha[:], z[:], ACT.Exp, scale=-1.0).then_inc(a_steps, 1)
                act.activation(small[:, :, H:3 * H], small[:, :, H:3 * H], ACT.Sqrt).then_inc(a_steps, 1)

        x1 = sb("x1_step", [B, D])
        vgb = sb("vgb_slots", [B, 2, 3 * D])
        gram = sb("gram_slots", [B, 2, 2 * D])
        key_row = sb("key_row", [B, H, N])
        query_row = sb("query_row", [B, H, N])
        prod = sb("prod", [B, 2, HD, N])
        pool_prod = sb("pool_prod", [B, 2, HD, N])
        sig = sb("sig", [B, 2 * D])
        rec = sb("rec", [B, H, HD])
        yv = rec
        ysq = sb("ysq", [B, H, HD])
        mean_sq = sb("mean_sq", [B, H])
        inv_rms = sb("inv_rms", [B, H])
        ctx_row = ysq[:].rearrange("b h e -> b (h e)")
        ctx_t = sb("ctx_t", [P, DC, B])
        x2 = sb("x2", [B, D])
        x2n = sb("x2n", [B, D])
        x2n_t = sb("x2n_t", [P, DC, B])
        acc = sb("acc", [B, D])
        stats = sb("stats2", [B, 6])
        mean_var = sb("mean_var2", [B, 2])
        var_eps = sb("var_eps2", [B, 1])
        rstd = sb("rstd2", [B, 1])
        logits = sb("logits", [B, E])
        best = sb("best", [B, E])
        best_at = sb("best_at", [B, E], U32)
        best_col = sb("best_col", [B, 2])
        lead = sb("lead", [B, 1])
        pair = sb("pair", [B, 2])
        share = sb("share", [B, 2, E])

        mix = ctx.enter_context(nc.psum_tensor("mix", [B, 4, D], F32))
        ctx_bank = ctx.enter_context(nc.psum_tensor("ctx_bank", [P, DC, B], F32))
        wo_bank = ctx.enter_context(nc.psum_tensor("wo_bank", [B, D], F32))
        x2n_bank = ctx.enter_context(nc.psum_tensor("x2n_bank", [P, DC, B], F32))
        logit_bank = ctx.enter_context(nc.psum_tensor("logit_bank", [B, D], F32))

        loaded = sem("step_loaded")
        x1_loaded = sem("x1_step_loaded")
        out_stored = sem("out_stored")
        sig_ready, key_row_ready, query_row_ready = sem("sig_ready"), sem("key_row_ready"), sem("query_row_ready")
        prod_ready, prod_free = sem("prod_ready"), sem("prod_free")
        delta_ready, y_ready, mean_sq_ready, inv_rms_ready = (sem(n) for n in (
            "delta_ready", "y_ready", "mean_sq_ready", "inv_rms_ready"))
        ctx_ready, ctx_turned, ctx_moved = sem("ctx_ready"), sem("ctx_turned"), sem("ctx_moved")
        wo_ready, x2_done, var_ready, rstd_ready = sem("wo_ready"), sem("x2_done"), sem("var2_ready"), sem("rstd2_ready")
        x2n_ready, x2n_turned, x2n_moved = sem("x2n_ready"), sem("x2n_turned"), sem("x2n_moved")
        logits_ready, logits_read, lead_ready, pair_ready = (sem(n) for n in (
            "logits_ready", "logits_read", "lead_ready", "pair_ready"))
        mix_ready, mix_free = sem("mix_ready"), sem("mix_free")
        combined = sem("combined")
        dve_steps, pool_steps = sem("vector_steps2"), sem("pool_steps2")
        block = ctx.enter_context(nc.Block())

        def slot(tensor, t):
            return tensor[:, bass.ds(t % 2, 1), :].rearrange("b a n -> b (a n)")

        def is_zero(t):
            return isinstance(t, int) and t == 0

        def heads(row, extent):
            return row.unsqueeze(2).to_broadcast([B, 2, HD, extent])

        def each_channel(per_head):
            return per_head.unsqueeze(2).to_broadcast([B, H, HD])

        def time_loop(eng, body):
            body(0, 8, True)
            for at in range(0, N, 8):
                with eng.Fori(max(at, 1), at + 8) as t:
                    body(t, at + 8, False)

        @block.sync
        def _(sp):
            def load(t):
                sp.dma_start(slot(vgb, t), vgb_d[:, bass.ds(t, 1), :].rearrange("b a n -> b (a n)"))\
                    .then_inc(loaded, 16)
                sp.dma_start(slot(gram, t).rearrange("b (w n) -> b w n", w=2),
                             gram_d[:, :, bass.ds(t, 1), :].rearrange("b w a n -> b w (a n)")).then_inc(loaded, 16)

            def load_x1(t):
                sp.dma_start(x1[:], x1_d[:, bass.ds(t, 1), :].rearrange("b a n -> b (a n)")).then_inc(x1_loaded, 16)

            def store(t):
                sp.wait_ge(combined, t + 1)
                sp.dma_start(out[:, bass.ds(t, 1), :].rearrange("b a n -> b (a n)"), acc[:]).then_inc(out_stored, 16)

            load(0)
            load_x1(0)
            sp.wait_ge(loaded, 32)
            load(1)
            with sp.Fori(1, N - 1) as t:
                sp.wait_ge(loaded, 32 * t + 32)
                sp.wait_ge(x2_done, t)
                load_x1(t)
                load(t + 1)
                store(t - 1)
            sp.wait_ge(x2_done, N - 1)
            load_x1(N - 1)
            store(N - 2)
            store(N - 1)
            sp.wait_ge(out_stored, 16 * N)

        @block.gpsimd
        def _(pool):
            own = Own(pool, pool_steps)

            def product(t, i, extent, row):
                h = 4 * (i % 8 // 2) + 2 + i % 2
                if not (is_zero(t) and i < 2):
                    pool.wait_ge(prod_free, 16 * t + i - 1)
                pool.tensor_tensor(pool_prod[:, i % 2, :, 0:extent],
                                   row[:, h:h + 1, 0:extent].to_broadcast([B, HD, extent]),
                                   deltas[:, h, :, 0:extent], ALU.mult).then_inc(prod_ready, 1)

            def norm_power(t):
                pool.wait_ge(var_ready, t + 1)
                pool.tensor_tensor(rstd[:], var_eps[:], half_off[:, 0:1], ALU.pow).then_inc(rstd_ready, 1)

            def row(dst, t, which, done):
                g = slot(gram, t)[:, which * D:which * D + D].rearrange("b (h s) -> b h s", h=H)
                own.then(pool.tensor_tensor(dst[:], g, decay[:], ALU.mult))
                inv = inv_norm[:, bass.ds(t, 1), which * H:which * H + H].rearrange("b a h -> b h a")
                pool.tensor_tensor(dst[:], dst[:], inv.to_broadcast([B, H, N]), ALU.mult).then_inc(done, 1)

            def body(t, extent, first):
                pool.wait_ge(loaded, 32 * t + 32)
                a = alpha[:, bass.ds(t, 1), :].rearrange("b a h -> b h a").to_broadcast([B, H, N])
                own.then(pool.tensor_tensor(decay[:], decay[:], a, ALU.mult))
                row(key_row, t, 0, key_row_ready)
                own.then(pool.tensor_copy(decay[:, :, bass.ds(t, 1)], ones[:].unsqueeze(2)))
                pool.wait_ge(key_row_ready, t + 1)
                if not first:
                    pool.wait_ge(delta_ready, t)
                product(t, 0, extent, key_row)
                if not first:
                    norm_power(t - 1)
                for i in range(1, 8):
                    product(t, i, extent, key_row)
                if not first:
                    pool.wait_ge(y_ready, t)
                row(query_row, t, 1, query_row_ready)
                pool.wait_ge(query_row_ready, t + 1)
                pool.wait_ge(delta_ready, t + 1)
                for i in range(8, 16):
                    product(t, i, extent, query_row)
                pool.wait_ge(mean_sq_ready, t + 1)
                pool.tensor_tensor(inv_rms[:], mean_sq[:], half_off[:], ALU.pow).then_inc(inv_rms_ready, 1)

            body(0, 8, True)
            for at in range(0, N, 8):
                with pool.Fori(max(at, 1), at + 8) as t:
                    own.turn(0, t, 4)
                    body(t, at + 8, False)
                    assert own.n == 4
            norm_power(N - 1)

        @block.scalar
        def _(act):
            with act.Fori(0, N) as t:
                act.wait_ge(loaded, 32 * t + 32)
                act.activation(sig[:], slot(vgb, t)[:, D:], ACT.Sigmoid).then_inc(sig_ready, 1)
                act.wait_ge(ctx_turned, t + 1)
                act.activation(ctx_t[:], ctx_bank[:], ACT.Copy).then_inc(ctx_moved, 1)
                act.wait_ge(x2n_turned, t + 1)
                act.activation(x2n_t[:], x2n_bank[:], ACT.Copy).then_inc(x2n_moved, 1)
                act.wait_ge(lead_ready, t + 1)
                act.activation(pair[:, 0:1], lead[:], ACT.Sigmoid)
                act.activation(pair[:, 1:2], lead[:], ACT.Sigmoid, scale=-1.0).then_inc(pair_ready, 1)

        @block.vector
        def _(dve):
            own = Own(dve, dve_steps, lambda: dve.tensor_copy(tick[:], half_off[:, 0:1]))

            def sums(t, dst, row, half, between):
                def chunks(extent):
                    summed = None
                    for c in range(H // 2):
                        hs = slice(2 * c, 2 * c + 2)
                        if c % 2 == 0:
                            if summed is not None:
                                own.wait(summed)
                            own.then(dve.tensor_tensor(prod[:, :, :, 0:extent], heads(row[:, hs, 0:extent], extent),
                                                       deltas[:, hs, :, 0:extent], ALU.mult))
                            summed = own.did(dve.tensor_reduce(dst[:, hs, :], prod[:, :, :, 0:extent], AX.X, ALU.add))
                        else:
                            for k in range(2):
                                i = 8 * half + c - 1 + k
                                dve.wait_ge(prod_ready, 16 * t + i + 1)
                                dve.tensor_reduce(dst[:, 2 * c + k, :], pool_prod[:, k, :, 0:extent], AX.X, ALU.add)\
                                    .then_inc(prod_free, 1)
                        if c in between:
                            between[c]()
                return chunks

            def residual(t):
                dve.wait_ge(wo_ready, t + 1)
                dve.wait_ge(x1_loaded, 16 * t + 16)
                dve.tensor_tensor(x2[:], wo_bank[:], x1[:], ALU.add).then_inc(x2_done, 1)
                dve.wait_ge(x2_done, t + 1)
                own.then(dve.tensor_tensor(x2[:], x2[:], bo_s[:], ALU.add))
                own.then_apart(dve.bn_stats(stats[:], x2[:]))
                own.then(dve.bn_aggr(mean_var[:], stats[:]))
                dve.tensor_scalar(var_eps[:], mean_var[:, 1:2], LN_EPS, None, ALU.add).then_inc(var_ready, 1)

            def normed(t):
                dve.wait_ge(rstd_ready, t + 1)
                dve.tensor_scalar(x2n[:], x2[:], mean_var[:, 0:1], rstd[:], ALU.subtract, ALU.mult)\
                    .then_inc(x2n_ready, 1)

            def route(t):
                dve.wait_ge(logits_ready, t + 1)
                dve.tensor_copy(logits[:], logit_bank[:, 0:E]).then_inc(logits_read, 1)
                wait_apart(dve, logits_read, t + 1)
                own.then(dve.max(best[:], logits[:]))
                dve.tensor_tensor(lead[:], best[:, 0:1], best[:, 1:2], ALU.subtract).then_inc(lead_ready, 1)
                own.then(dve.max_index(best_at[:], best[:], logits[:]))
                own.then(dve.tensor_copy(best_col[:], best_at[:, 0:2]))

            def shares(t):
                dve.wait_ge(pair_ready, t + 1)
                for i in range(2):
                    c = own.did(dve.tensor_scalar(share[:, i, :], column[:], best_col[:, i:i + 1], pair[:, i:i + 1],
                                                  ALU.is_equal, ALU.mult))
                own.wait(c)
                own.then(dve.tensor_tensor(share[:, 0, :], share[:, 0, :], share[:, 1, :], ALU.add))

            def combine(t, e):
                dve.wait_ge(mix_ready, 8 * t + e + 1)
                if e == 0 and not is_zero(t):
                    dve.wait_ge(out_stored, 16 * t)
                if e > 0:
                    dve.wait_ge(mix_free, 7 * t + e)
                dve.scalar_tensor_tensor(acc[:], mix[:, e % 4, :], share[:, 0, e:e + 1], x2[:] if e == 0 else acc[:],
                                         ALU.mult, ALU.add).then_inc(combined if e == E - 1 else mix_free, 1)

            def body(t, extent, first):
                early, late = {}, {}
                if not first:
                    early = {0: lambda: residual(t - 1), 3: lambda: normed(t - 1), 6: lambda: route(t - 1)}
                    late = {c: (lambda e: lambda: combine(t - 1, e))(c) for c in range(E)}
                dve.wait_ge(key_row_ready, t + 1)
                sums(t, rec, key_row, 0, early)(extent)
                dve.wait_ge(prod_free, 16 * t + 8)
                own.wait(own.base + own.n)
                v = slot(vgb, t)[:, 0:D].rearrange("b (h e) -> b h e", h=H)
                own.then(dve.tensor_tensor(rec[:], v, rec[:], ALU.subtract))
                dve.wait_ge(sig_ready, t + 1)
                own.then(dve.tensor_tensor(rec[:], rec[:], sig[:, D:].rearrange("b (h e) -> b h e", h=H), ALU.mult))
                inv = inv_norm[:, bass.ds(t, 1), 0:H].rearrange("b a h -> b h a")
                dve.tensor_tensor(deltas[:, :, :, bass.ds(t, 1)], rec[:].unsqueeze(3),
                                  inv.unsqueeze(2).to_broadcast([B, H, HD, 1]), ALU.mult).then_inc(delta_ready, 1)
                if not first:
                    shares(t - 1)
                dve.wait_ge(delta_ready, t + 1)
                dve.wait_ge(query_row_ready, t + 1)
                sums(t, yv, query_row, 1, late)(extent)
                dve.wait_ge(prod_free, 16 * t + 16)
                own.wait(own.base + own.n)
                dve.tensor_tensor(ysq[:], yv[:], yv[:], ALU.mult).then_inc(y_ready, 1)
                dve.wait_ge(y_ready, t + 1)
                own.then(dve.tensor_reduce(mean_sq[:], ysq[:], AX.X, ALU.add))
                dve.tensor_scalar(mean_sq[:], mean_sq[:], 1.0 / HD, RMS_EPS, ALU.mult, ALU.add).then_inc(mean_sq_ready, 1)
                own.then(dve.tensor_tensor(ysq[:], yv[:], sig[:, 0:D].rearrange("b (h e) -> b h e", h=H), ALU.mult))
                g = slot(vgb, t)[:, D:2 * D].rearrange("b (h e) -> b h e", h=H)
                own.then(dve.tensor_tensor(ysq[:], ysq[:], g, ALU.mult))
                own.then(dve.tensor_tensor(ysq[:], ysq[:], normw[:].unsqueeze(1).to_broadcast([B, H, HD]), ALU.mult))
                dve.wait_ge(inv_rms_ready, t + 1)
                dve.tensor_tensor(ctx_row[:].rearrange("b (h e) -> b h e", h=H), ysq[:], each_channel(inv_rms[:]),
                                  ALU.mult).then_inc(ctx_ready, 1)

            body(0, 8, True)
            before = own.n
            own.turn(before, 0, 0)
            per_turn = VECTOR_STEPS
            for at in range(0, N, 8):
                with dve.Fori(max(at, 1), at + 8) as t:
                    own.turn(before, t - 1, per_turn)
                    body(t, at + 8, False)
                    assert own.n == per_turn, own.n
            own.turn(before + (N - 1) * per_turn, 0, 0)
            residual(N - 1)
            normed(N - 1)
            route(N - 1)
            shares(N - 1)
            for e in range(E):
                combine(N - 1, e)

        @block.tensor
        def _(pe):
            def body(t, first):
                pe.wait_ge(ctx_ready, t + 1)
                for c in range(DC):
                    last = pe.transpose(ctx_bank[:, c, :], ctx_row[:, c * P:c * P + P], ident[0:B, 0:B])
                last.then_inc(ctx_turned, 1)
                pe.wait_ge(ctx_moved, t + 1)
                if not first:
                    pe.wait_ge(x2_done, t)
                products(pe, wo_bank[:], [(ctx_t[:, c, :], wo[:, c, :]) for c in range(DC)]).then_inc(wo_ready, 1)
                pe.wait_ge(x2n_ready, t + 1)
                for c in range(DC):
                    last = pe.transpose(x2n_bank[:, c, :], x2n[:, c * P:c * P + P], ident[0:B, 0:B])
                last.then_inc(x2n_turned, 1)
                pe.wait_ge(x2n_moved, t + 1)
                if not first:
                    pe.wait_ge(logits_read, t)
                products(pe, logit_bank[:, 0:E], [(x2n_t[:, c, :], gate[:, c, :]) for c in range(DC)]).then_inc(logits_ready, 1)
                for e in range(E):
                    if e < 4:
                        if not first:
                            pe.wait_ge(mix_free, 7 * (t - 1) + min(e + 5, 7))
                            if e == 3:
                                pe.wait_ge(combined, t)
                    else:
                        pe.wait_ge(mix_free, 7 * t + e - 3)
                    products(pe, mix[:, e % 4, :], [(x2n_t[:, c, :], experts[:, e, c, :]) for c in range(DC)])\
                        .then_inc(mix_ready, 1)

            body(0, True)
            with pe.Fori(1, N) as t:
                body(t, False)


VECTOR_STEPS = 32

INPUTS = ["x", "cond_t", "cond_last_t", "q_w", "q_b", "kv_w", "kv_b", "proj_w", "proj_b", "attn_w_t", "wa_t",
          "dt_bias", "a_log", "norm_w", "wo_t", "bo", "gate_t", "expert_t"]


def laid_out(x, ctx_768, L0_xattn_q_w, L0_xattn_q_b, L0_xattn_kv_w, L0_xattn_kv_b, L0_xattn_proj_w, L0_xattn_proj_b,
             L0_attn_Wq, L0_attn_Wk, L0_attn_Wv, L0_attn_Wg, L0_attn_Wb, L0_attn_Wa, L0_attn_dt_bias, L0_attn_A_log,
             L0_attn_norm_w, L0_attn_Wo, L0_attn_bo, L0_ffn_gate_w, L0_ffn_expert_w):
    import numpy as np

    ctx = np.asarray(ctx_768)
    arrays = [x, ctx.transpose(2, 0, 1).reshape(C, B * M), ctx[:, M - 1, :].T, L0_xattn_q_w,
              np.asarray(L0_xattn_q_b).reshape(-1, P).T, L0_xattn_kv_w,
              np.asarray(L0_xattn_kv_b).reshape(-1, P).T, L0_xattn_proj_w, L0_xattn_proj_b,
              np.stack([np.asarray(w).T for w in (L0_attn_Wq, L0_attn_Wk, L0_attn_Wv, L0_attn_Wg, L0_attn_Wb)]),
              np.asarray(L0_attn_Wa).T, L0_attn_dt_bias, L0_attn_A_log, L0_attn_norm_w, np.asarray(L0_attn_Wo).T,
              L0_attn_bo, np.asarray(L0_ffn_gate_w).T, np.asarray(L0_ffn_expert_w).transpose(0, 2, 1)]
    return {name: np.ascontiguousarray(a) for name, a in zip(INPUTS, arrays)}


def kernel(**inputs):
    import concourse.bacc as bacc
    from concourse.bass_utils import run_bass_kernel_spmd

    arrays = laid_out(**inputs)
    nc = bacc.Bacc("TRN2", target_bir_lowering=False, num_devices=1)
    args = [nc.dram_tensor(f"{name}_dram", a.shape, mybir.dt.from_np(a.dtype), kind="ExternalInput").ap()
            for name, a in arrays.items()]
    out = nc.dram_tensor("out", [B, N, D], F32, kind="ExternalOutput").ap()
    build(nc, *args, out)
    result = run_bass_kernel_spmd(nc, [{f"{name}_dram": a for name, a in arrays.items()}], core_ids=[0])
    return result.results[0]["out"]
```

```python
import concourse.bass as bass
import concourse.mybir as mybir
from concourse.alu_op_type import AluOpType as ALU
from contextlib import ExitStack, nullcontext

ACT = mybir.ActivationFunctionType
AX = mybir.AxisListType
F32 = mybir.dt.float32
F32R = mybir.dt.float32r
U32 = mybir.dt.uint32

B, N, D = 128, 32, 512
M, C = 257, 384
H, HD = 16, 32
E = 8
P = 128
BU = P // N
NU = B // BU
DC, CC = D // P, C // P
HG = H // 4
MU = BU * M
KEYS = (P, M - 1 - P)
PIECES = ((0, 344), (344, 342), (686, 342))
SHARED = H // 2
EARLY = 16
SCALE = HD ** -0.5
LN_EPS, RMS_EPS = 1e-5, 1e-6


class Ring:

    A = ["K00", "K01", "K02", "K03", "K10", "K11", "K12", "K13", "XT", "K20", "K21", "K22", "K23", "QT",
         "V00", "V01", "L0", "O0", "V10", "V11", "L1", "O1", "V20", "V21", "L2", "O2", "V30", "V31", "L3",
         "O3", "PR"]
    BOTH = ["K00", "K01", "K02", "K03", "X1T", "K10", "K11", "KK", "QQ", "K12", "K13", "XT", "K20", "K21",
            "V2", "BT", "GT", "AL", "K22", "K23", "QT", "D0", "D1"] + A[14:29] + ["D2", "O3", "D3", "PR"]
    B = ["X1T", "KK", "QQ", "V2", "BT", "GT", "AL", "D0", "D1", "D2", "D3"]

    def __init__(self, full, free):
        self.full, self.free = full, free
        assert len(self.BOTH) % 2 == 0

    def use(self, name, u):
        if isinstance(u, int) and u == 0:
            n = self.A.index(name)
            return n % 2, n // 2
        if isinstance(u, int) and u == NU:
            n = len(self.A) + (NU - 1) * len(self.BOTH) + self.B.index(name)
            return n % 2, n // 2
        n = len(self.A) + self.BOTH.index(name)
        return n % 2, (u - 1) * (len(self.BOTH) // 2) + n // 2

    def claim(self, pe, name, u):
        bank, before = self.use(name, u)
        if not (isinstance(before, int) and before == 0):
            pe.wait_ge(self.free[bank], before)
        return bank

    def wait_full(self, eng, name, u):
        bank, before = self.use(name, u)
        eng.wait_ge(self.full[bank], before + 1)
        return bank

    def wait_read(self, eng, name, u):
        bank, before = self.use(name, u)
        eng.wait_ge(self.free[bank], before + 1)


def merged(first, second):
    tasks, done = [], 0
    for i, task in enumerate(first):
        until = len(second) * (i + 1) // len(first)
        tasks += [task] + second[done:until]
        done = until
    return tasks + second[done:]


def wait_apart(eng, sem, count):
    eng.wait_ge(sem, 1)
    eng.wait_ge(sem, count)


class Own:

    def __init__(self, eng, sem, carrier=None):
        self.eng, self.sem, self.carrier, self.base, self.n = eng, sem, carrier, 0, 0

    def did(self, ins):
        ins.then_inc(self.sem, 1)
        self.n += 1
        return self.base + self.n

    def wait(self, count):
        self.eng.wait_ge(self.sem, count)

    def then(self, ins):
        self.wait(self.did(ins))

    def then_apart(self, ins):
        self.then(ins)
        self.did(self.carrier())

    def turn(self, start, number, per_turn):
        self.base, self.n = start + number * per_turn, 0


def split_exactly(eng, own, high, low, whole):
    own.then(eng.tensor_copy(high, whole))
    return eng.tensor_tensor(low, whole, high.bitcast(F32), ALU.subtract)


def products(pe, out, terms):
    for i, (lhs_t, rhs) in enumerate(terms):
        last = pe.matmul(out, lhs_t, rhs, start=(i == 0), stop=(i == len(terms) - 1))
    return last


def split_terms(lhs_t, rhs):
    (lh, ll), (rh, rl) = lhs_t, rhs
    return [(lh, rh), (lh, rl), (ll, rh)]


def build(nc, x, cond_t, cond_last_t, q_w, q_b, kv_w, kv_b, proj_w, proj_b, attn_w_t, wa_t, dt_bias, a_log,
          norm_w, wo_t, bo, gate_t, expert_t, out):
    v_last_d = nc.dram_tensor("v_last", [B, D], F32).ap()
    x1_d = nc.dram_tensor("x1_rows", [B, N, D], F32).ap()
    vgb_d = nc.dram_tensor("vgb_rows", [B, N, 3 * D], F32).ap()
    small_d = nc.dram_tensor("small_rows", [B, N, 3 * H], F32).ap()
    gram_d = nc.dram_tensor("gram_rows", [B, 2, N, D], F32).ap()
    with ExitStack() as both:
        ident = both.enter_context(nc.sbuf_tensor("ident", [P, P], F32))
        cross_pass(nc, ident, x, cond_t, cond_last_t, q_w, q_b, kv_w, kv_b, proj_w, proj_b, attn_w_t, wa_t,
                   norm_w, v_last_d, x1_d, vgb_d, small_d, gram_d)
        time_pass(nc, ident, x1_d, vgb_d, small_d, gram_d, dt_bias, a_log, wo_t, bo, gate_t,
                  expert_t, out)


def cross_pass(nc, ident, x, cond_t, cond_last_t, q_w, q_b, kv_w, kv_b, proj_w, proj_b, attn_w_t, wa_t,
               norm_w, v_last_d, x1_d, vgb_d, small_d, gram_d):
    with ExitStack() as ctx:
        def sb(name, shape, dt=F32):
            return ctx.enter_context(nc.sbuf_tensor(name, shape, dt))

        def sem(name):
            return ctx.enter_context(nc.semaphore(name))

        wq = sb("wq", [P, DC, D])
        wkv_high = sb("wkv_high", [P, CC, 2 * D], F32R)
        wkv_low = sb("wkv_low", [P, CC, 2 * D], F32R)
        wproj = sb("wproj", [P, HG, D])
        wattn = sb("wattn", [P, 5, DC, D])
        wa = sb("wa", [P, DC, H])
        qb = sb("qb", [P, HG])
        kvb = sb("kvb", [P, 2 * HG])
        projb = sb("projb", [P, D])
        head_of = sb("head_of", [P, HG, H])

        cond = sb("cond", [P, CC, MU])
        cond_high = sb("cond_high", [P, CC, MU], F32R)
        cond_low = sb("cond_low", [P, CC, MU], F32R)
        x_in = sb("x_in", [P, D])
        x_res = sb("x_res", [P, D])
        xn = sb("xn", [P, D])
        xn_t = sb("xn_t", [P, DC, P])
        q_s = sb("q_s", [P, HG, P])
        q_diag = sb("q_diag", [P, HG * BU, P])
        k_t = sb("k_t", [P, HG, MU])
        v_s = sb("v_s", [P, 2, D])
        v_last = sb("v_last_s", [HG, BU, P])
        prob = sb("prob", [P, HG, M])
        prob_t = sb("prob_t", [P, 2, HG * P])
        prob_last_t = sb("prob_last_t", [HG, HG, P])
        neg_max = sb("neg_max", [P, HG])
        sums = sb("sums", [P, HG])
        inv_sums = sb("inv_sums", [P, HG])
        att_t = sb("att_t", [P, HG, P])
        x1 = sb("x1", [P, D])
        x1n = sb("x1n", [P, D])
        x1n_t = sb("x1n_t", [P, DC, P])
        kq = sb("kq", [P, HG * BU, 2 * N])
        k_diag = sb("k_diag", [P, HG * BU, P])
        squares = sb("squares", [P, 2, D])
        vgb = sb("vgb", [P, 4, D])
        normw = sb("normw", [P, HD])
        small = sb("small", [P, 3 * H])
        gram = sb("gram", [2 * N, 2, D])
        stats = sb("stats", [P, 6])
        mean_var = sb("mean_var", [P, 2])
        var_eps = sb("var_eps", [P, 2])
        rstd = sb("rstd", [P, 2])
        minus_half = sb("minus_half", [P, 1])
        tick, tick_v = sb("tick", [P, 1]), sb("tick_v", [P, 1])

        with ExitStack() as pre:
            wkv = k_t[:].rearrange("p g n -> p (g n)")[:, 0:CC * 2 * D].rearrange("p (c n) -> p c n", c=CC)
            cond_last = cond[:, :, 0:B]
            v_last_all = x1[0:B, :]
            bank = pre.enter_context(nc.psum_tensor("v_last_bank", [B, D], F32))
            loaded = pre.enter_context(nc.semaphore("weights_loaded"))
            kv_loaded = pre.enter_context(nc.semaphore("kv_loaded"))
            pool_own = pre.enter_context(nc.semaphore("setup_pool_steps"))
            dve_own = pre.enter_context(nc.semaphore("setup_vector_steps"))
            v_last_ready = pre.enter_context(nc.semaphore("v_last_ready"))
            v_last_moved = pre.enter_context(nc.semaphore("v_last_moved"))
            v_last_stored = pre.enter_context(nc.semaphore("v_last_stored"))
            block = pre.enter_context(nc.Block())

            @block.sync
            def _(sp):
                sp.dma_start(wkv, kv_w.rearrange("(c p) n -> p c n", p=P)).then_inc(kv_loaded, 16)
                sp.dma_start(cond_last, cond_last_t.rearrange("(c p) n -> p c n", p=P)).then_inc(kv_loaded, 16)
                loads = [(wq[:], q_w.rearrange("(c p) n -> p c n", p=P)),
                         (wproj[:], proj_w.rearrange("(c p) n -> p c n", p=P)),
                         (qb[:], q_b),
                         (kvb[:], kv_b),
                         (normw[:], norm_w.rearrange("(a n) -> a n", a=1).to_broadcast([P, HD])),
                         (projb[:], proj_b.rearrange("(a n) -> a n", a=1).to_broadcast([P, D]))]
                for dst, src in loads:
                    sp.dma_start(dst, src).then_inc(loaded, 16)
                sp.wait_ge(v_last_moved, 1)
                sp.dma_start(v_last_d, v_last_all).then_inc(v_last_stored, 16)
                sp.wait_ge(v_last_stored, 16)
                sp.wait_ge(loaded, 16 * len(loads))

            @block.gpsimd
            def _(pool):
                own = Own(pool, pool_own)
                own.did(pool.memset(minus_half[:], -0.5))
                own.did(pool.memset(q_diag[:], 0.0))
                own.did(pool.memset(k_diag[:], 0.0))
                own.did(pool.memset(head_of[:], 1.0))
                own.then(pool.memset(ident[:], 0.0))
                own.did(pool.affine_select(out=ident[:], in_=ident[:], compare_op=ALU.not_equal, fill=1.0, base=0,
                                           pattern=[[-1, P]], channel_multiplier=1))
                own.then(pool.affine_select(out=head_of[:], in_=head_of[:], compare_op=ALU.is_ge, fill=0.0,
                                            base=0, pattern=[[P, HG], [-HD, H]], channel_multiplier=1))
                own.then(pool.affine_select(out=head_of[:], in_=head_of[:], compare_op=ALU.is_ge, fill=0.0,
                                            base=HD - 1, pattern=[[-P, HG], [HD, H]], channel_multiplier=-1))

            @block.vector
            def _(dve):
                own = Own(dve, dve_own)
                dve.wait_ge(kv_loaded, 32)
                own.then(split_exactly(dve, own, wkv_high[:], wkv_low[:], wkv))
                dve.wait_ge(v_last_ready, 1)
                dve.tensor_copy(v_last_all, bank[:]).then_inc(v_last_moved, 1)

            @block.tensor
            def _(pe):
                pe.wait_ge(kv_loaded, 32)
                products(pe, bank[:], [(cond_last[:, c, :], wkv[:, c, D:]) for c in range(CC)]).then_inc(v_last_ready, 1)

        ring_bank = [ctx.enter_context(nc.psum_tensor(f"ring{i}", [P, D], F32)) for i in range(2)]
        score = ctx.enter_context(nc.psum_tensor("score", [P, HG, D], F32))
        turned = [ctx.enter_context(nc.psum_tensor(f"turned{i}", [P, HG * P], F32)) for i in range(2)]

        ring = Ring([sem("ring0_full"), sem("ring1_full")], [sem("ring0_free"), sem("ring1_free")])
        attn_loaded = sem("attn_loaded")
        cond_loaded, x_loaded, v_last_loaded = sem("cond_loaded"), sem("x_loaded"), sem("v_last_loaded")
        x_used = sem("x_used")
        split_done = sem("split_done")
        var_ready, rstd_ready = sem("var_ready"), sem("rstd_ready")
        xn_ready, x1n_ready = sem("xn_ready"), sem("x1n_ready")
        q_diag_ready = sem("q_diag_ready")
        score_ready, neg_max_ready = sem("score_ready"), sem("neg_max_ready")
        exp_done, prob_ready = sem("exp_done"), sem("prob_ready")
        turned_ready, prob_t0_ready, prob_t1_ready = sem("turned_ready"), sem("prob_t0_ready"), sem("prob_t1_ready")
        kq_ready, k_diag_ready = sem("kq_ready"), sem("k_diag_ready")
        vgb_ready = sem("vgb_ready")
        x1_stored, vgb_stored, small_stored = sem("x1_stored"), sem("vgb_stored"), sem("small_stored")
        gram_stored = [sem("gram0_stored"), sem("gram1_stored")]
        dve_steps, pool_steps = sem("vector_steps"), sem("pool_steps")

        block = ctx.enter_context(nc.Block())
        rows_x = x.rearrange("b t n -> (b t) n")
        rows_x1 = x1_d.rearrange("b t n -> (b t) n")
        rows_vgb = vgb_d.rearrange("b t n -> (b t) n")
        rows_small = small_d.rearrange("b t n -> (b t) n")
        rows_gram = gram_d.rearrange("b w t n -> (b w t) n")
        cond_v = cond_t.rearrange("(c p) n -> p c n", p=P)

        @block.sync
        def _(sp):
            def load_cond(u):
                if not (isinstance(u, int) and u == 0):
                    sp.wait_ge(split_done, u * BU)
                sp.dma_start(cond[:], cond_v[:, :, bass.ds(u * MU, MU)]).then_inc(cond_loaded, 16)

            def load_x(u):
                if not (isinstance(u, int) and u == 0):
                    sp.wait_ge(x_used, u)
                sp.dma_start(x_in[:], rows_x[bass.ds(u * P, P), :]).then_inc(x_loaded, 16)

            def load_v_last(u):
                if not (isinstance(u, int) and u == 0):
                    ring.wait_full(sp, "PR", u - 1)
                sp.dma_start(v_last[:], v_last_d[bass.ds(u * BU, BU), :].rearrange("b (g j) -> g b j", g=HG))\
                    .then_inc(v_last_loaded, 16)

            def store_results(u):
                sp.wait_ge(vgb_ready, u)
                sp.dma_start(rows_vgb[bass.ds((u - 1) * P, P), :], vgb[:, 0:3].rearrange("p a n -> p (a n)"))\
                    .then_inc(vgb_stored, 16)
                ring.wait_read(sp, "AL", u)
                sp.dma_start(rows_small[bass.ds((u - 1) * P, P), :], small[:]).then_inc(small_stored, 16)
                for b in range(BU):
                    ring.wait_read(sp, f"D{b}", u)
                    sp.dma_start(rows_gram[bass.ds(((u - 1) * BU + b) * 2 * N, 2 * N), :], gram[:, b % 2, :])\
                        .then_inc(gram_stored[b % 2], 16)

            def store_x1(u):
                ring.wait_read(sp, "PR", u - 1)
                sp.dma_start(rows_x1[bass.ds((u - 1) * P, P), :], x1[:]).then_inc(x1_stored, 16)

            load_x(0)
            load_cond(0)
            load_v_last(0)
            sp.dma_start(wa[:], wa_t.rearrange("(c p) n -> p c n", p=P)).then_inc(attn_loaded, 16)
            for i in range(5):
                sp.dma_start(wattn[:, i], attn_w_t[i].rearrange("(c p) n -> p c n", p=P)).then_inc(attn_loaded, 16)
            load_cond(1)
            load_x(1)
            with sp.Fori(1, NU - 1) as u:
                store_x1(u)
                load_v_last(u)
                load_cond(u + 1)
                load_x(u + 1)
                store_results(u)
            store_x1(NU - 1)
            load_v_last(NU - 1)
            store_results(NU - 1)
            store_x1(NU)
            store_results(NU)
            for done, n in ((x1_stored, NU), (vgb_stored, NU), (small_stored, NU),
                            (gram_stored[0], 2 * NU), (gram_stored[1], 2 * NU)):
                sp.wait_ge(done, 16 * n)

        @block.gpsimd
        def _(pool):
            own = Own(pool, pool_steps, lambda: pool.tensor_tensor(tick[:], minus_half[:], minus_half[:], ALU.add))

            def split(u):
                pool.wait_ge(cond_loaded, 16 * u + 16)
                for b in range(BU):
                    if not (isinstance(u, int) and u == 0):
                        ring.wait_full(pool, f"V{b}1", u - 1)
                        own.did(own.carrier())
                    cols = slice(b * M, (b + 1) * M)
                    split_exactly(pool, own, cond_high[:, :, cols], cond_low[:, :, cols], cond[:, :, cols])\
                        .then_inc(split_done, 1)

            def norm_power(i, count):
                pool.wait_ge(var_ready, count)
                pool.tensor_tensor(rstd[:, i:i + 1], var_eps[:, i:i + 1], minus_half[:], ALU.pow).then_inc(rstd_ready, 1)

            split(0)
            norm_power(0, 1)
            split(1)
            norm_power(1, 2)
            with pool.Fori(1, NU - 1) as u:
                own.turn(3 * BU, u - 1, 2 * BU)
                norm_power(0, 2 * u + 1)
                split(u + 1)
                assert own.n == 2 * BU
                norm_power(1, 2 * u + 2)
            norm_power(0, 2 * (NU - 1) + 1)
            norm_power(1, 2 * (NU - 1) + 2)

        @block.scalar
        def _(act):
            def move(name, u, dst, func=ACT.Copy, **how):
                bank = ring.wait_full(act, name, u)
                act.activation(dst, ring_bank[bank][:], func, **how).then_inc(ring.free[bank], 1)

            def move_keys(u, piece, group):
                bank = ring.wait_full(act, f"K{piece}{group}", u)
                at, n = PIECES[piece]
                act.activation(k_t[:, group, at:at + n], ring_bank[bank][:, 0:n], ACT.Identity,
                               bias=kvb[:, group:group + 1]).then_inc(ring.free[bank], 1)

            def move_kq(u, i, name):
                bank = ring.wait_full(act, name, u)
                act.activation(kq[:, :, i * N:i * N + N], ring_bank[bank][:].rearrange("p (g t) -> p g t", t=N),
                               ACT.Copy).then_inc(kq_ready, 1)
                act.activation(squares[:, i, :], ring_bank[bank][:], ACT.Square).then_inc(ring.free[bank], 1)

            def move_gram(u, b):
                if not (isinstance(u, int) and u == 1 and b < 2):
                    act.wait_ge(gram_stored[b % 2], ((u - 1) * 2 + b // 2) * 16)
                bank = ring.wait_full(act, f"D{b}", u)
                act.activation(gram[:, b % 2, :], ring_bank[bank][0:2 * N, :], ACT.Copy)\
                    .then_inc(ring.free[bank], 1)

            def turn(u, first=False, last=False):
                a, b_ = not last, not first
                if a:
                    for g in range(4):
                        move_keys(u, 0, g)
                if b_:
                    move("X1T", u, x1n_t[:].rearrange("p c t -> p (c t)"))
                if a:
                    move_keys(u, 1, 0)
                    move_keys(u, 1, 1)
                if b_:
                    move_kq(u, 0, "KK")
                    move_kq(u, 1, "QQ")
                    act.wait_ge(kq_ready, 2 * u)
                    for h in range(4):
                        rows = slice(HD * h, HD * h + HD)
                        ins = act.activation(k_diag[rows, :, HD * h:HD * h + HD], kq[rows, :, 0:N], ACT.Copy)
                    ins.then_inc(k_diag_ready, 1)
                if a:
                    move_keys(u, 1, 2)
                    move_keys(u, 1, 3)
                    move("XT", u, xn_t[:].rearrange("p c t -> p (c t)"))
                    move_keys(u, 2, 0)
                    move_keys(u, 2, 1)
                if b_:
                    wait_stored(act, vgb_stored, u)
                    move("V2", u, vgb[:, 0, :])
                    move("BT", u, vgb[:, 2, :], func=ACT.Exp, scale=-1.0)
                    bank = ring.wait_full(act, "GT", u)
                    act.activation(vgb[:, 1, :], ring_bank[bank][:], ACT.Copy)
                    act.activation(vgb[:, 3, :], ring_bank[bank][:], ACT.Exp, scale=-1.0).then_inc(ring.free[bank], 1)
                    wait_stored(act, small_stored, u)
                    bank = ring.wait_full(act, "AL", u)
                    act.activation(small[:], ring_bank[bank][:, 0:3 * H], ACT.Copy).then_inc(ring.free[bank], 1)
                if a:
                    move_keys(u, 2, 2)
                    move_keys(u, 2, 3)
                if b_:
                    for b in range(BU if last else 2):
                        move_gram(u, b)
                if a:
                    for b in range(BU):
                        n = u * BU + b
                        act.wait_ge(neg_max_ready, n + 1)
                        for g in range(HG):
                            act.activation(prob[:, g, :], score[:, g, 0:M], ACT.Exp, bias=neg_max[:, g:g + 1],
                                           accum_out=sums[:, g:g + 1]).then_inc(exp_done, 1)
                        move(f"V{b}0", u, v_s[:, 0, :])
                        move(f"V{b}1", u, v_s[:, 1, :])
                        act.wait_ge(turned_ready, n + 1)
                        act.activation(prob_t[:, 0, :], turned[0][:], ACT.Copy).then_inc(prob_t0_ready, 1)
                    if b_:
                        move_gram(u, 2)
                        move_gram(u, 3)

            def wait_stored(eng, stored, u):
                if not (isinstance(u, int) and u == 1):
                    eng.wait_ge(stored, (u - 1) * 16)

            turn(0, first=True)
            turn(1)
            with act.Fori(2, NU) as u:
                turn(u)
            turn(NU, last=True)

        @block.vector
        def _(dve):
            own = Own(dve, dve_steps, lambda: dve.tensor_copy(tick_v[:], minus_half[:]))

            def norm(rows, i, count, dst):
                own.then_apart(dve.bn_stats(stats[:], rows))
                own.then(dve.bn_aggr(mean_var[:], stats[:]))
                dve.tensor_scalar(var_eps[:, i:i + 1], mean_var[:, 1:2], LN_EPS, None, ALU.add).then_inc(var_ready, 1)
                dve.wait_ge(rstd_ready, count)
                return dve.tensor_scalar(dst, rows, mean_var[:, 0:1], rstd[:, i:i + 1], ALU.subtract, ALU.mult)

            def gates(u):
                ring.wait_read(dve, "GT", u)
                own.then(dve.tensor_scalar(vgb[:, 2:4], vgb[:, 2:4], 1.0, None, ALU.add))
                own.then(dve.reciprocal(vgb[:, 2:4], vgb[:, 2:4]))
                own.then(dve.tensor_tensor(vgb[:, 1], vgb[:, 1], vgb[:, 3], ALU.mult))
                by_head = vgb[:, 1].rearrange("p (h e) -> p h e", h=H)
                dve.tensor_tensor(by_head, by_head, normw[:].unsqueeze(1).to_broadcast([P, H, HD]), ALU.mult)\
                    .then_inc(vgb_ready, 1)

            def turn(u):
                n0 = u * BU
                first = isinstance(u, int) and u == 0
                dve.wait_ge(x_loaded, 16 * u + 16)
                norm(x_in[:], 0, 2 * u + 1, xn[:]).then_inc(xn_ready, 1)
                dve.tensor_tensor(x_res[:], x_in[:], projb[:], ALU.add).then_inc(x_used, 1)
                if not first:
                    gates(u)
                bank = ring.wait_full(dve, "QT", u)
                own.then(dve.tensor_tensor(q_s[:], ring_bank[bank][:].rearrange("p (g t) -> p g t", g=HG),
                                           qb[:].unsqueeze(2).to_broadcast([P, HG, P]), ALU.add))
                for h in range(4):
                    rows = slice(HD * h, HD * h + HD)
                    src = q_s[rows].rearrange("p g (b t) -> p (g b) t", t=N)
                    last = dve.tensor_scalar(q_diag[rows, :, HD * h:HD * h + HD], src, SCALE, None, ALU.mult)
                    if h == 0:
                        last.then_inc(ring.free[bank], 1)
                last.then_inc(q_diag_ready, 1)

                def maximum(b):
                    dve.wait_ge(score_ready, n0 + b + 1)
                    dve.tensor_reduce(neg_max[:], score[:, :, 0:M], AX.X, ALU.max, negate=True)\
                        .then_inc(neg_max_ready, 1)

                def normalise(b):
                    dve.wait_ge(exp_done, (n0 + b + 1) * HG)
                    own.then(dve.reciprocal(inv_sums[:], sums[:]))
                    for g in range(HG):
                        last = dve.tensor_scalar(prob[:, g, :], prob[:, g, :], inv_sums[:, g:g + 1], None, ALU.mult)
                    last.then_inc(prob_ready, 1)

                def move_turned(b):
                    dve.wait_ge(turned_ready, n0 + b + 1)
                    dve.tensor_copy(prob_t[:, 1, :], turned[1][:]).then_inc(prob_t1_ready, 1)
                    bank = ring.wait_full(dve, f"L{b}", u)
                    dve.tensor_tensor(prob_last_t[:],
                                      ring_bank[bank][0:HG, 0:P].unsqueeze(1).to_broadcast([HG, HG, P]),
                                      ident[0:HG, 0:HG].unsqueeze(2).to_broadcast([HG, HG, P]), ALU.mult)\
                        .then_inc(ring.free[bank], 1)

                def move_attended(b):
                    bank = ring.wait_full(dve, f"O{b}", u)
                    for h in range(4):
                        rows = slice(HD * h, HD * h + HD)
                        src = ring_bank[bank][rows, :].rearrange("p (g t) -> p g t", g=HG)[:, :, HD * h:HD * h + HD]
                        last = dve.tensor_tensor(att_t[rows, :, b * N:b * N + N], src,
                                                 kvb[rows, HG:].unsqueeze(2).to_broadcast([HD, HG, N]), ALU.add)
                    last.then_inc(ring.free[bank], 1)

                maximum(0)
                normalise(0)
                move_turned(0)
                for b in range(1, BU):
                    maximum(b)
                    move_attended(b - 1)
                    normalise(b)
                    move_turned(b)
                move_attended(BU - 1)
                bank = ring.wait_full(dve, "PR", u)
                if not first:
                    dve.wait_ge(x1_stored, 16 * u)
                dve.tensor_tensor(x1[:], ring_bank[bank][:], x_res[:], ALU.add).then_inc(ring.free[bank], 1)
                ring.wait_read(dve, "PR", u)
                norm(x1[:], 1, 2 * u + 2, x1n[:]).then_inc(x1n_ready, 1)

            turn(0)
            before = own.n
            per_turn = before + 3
            with dve.Fori(1, NU) as u:
                own.turn(before, u - 1, per_turn)
                turn(u)
                assert own.n == per_turn
            own.turn(before + (NU - 1) * per_turn, 0, 0)
            gates(NU)

        @block.tensor
        def _(pe):
            def bank_of(name, u):
                bank = ring.claim(pe, name, u)
                return ring_bank[bank], ring.full[bank]

            def keys(u, piece, group):
                at, n = PIECES[piece]
                if group == 0:
                    pe.wait_ge(split_done, u * BU + piece + 2)
                bank, full = bank_of(f"K{piece}{group}", u)
                terms = []
                for c in range(CC):
                    w = slice(group * P, group * P + P)
                    terms += split_terms((wkv_high[:, c, w], wkv_low[:, c, w]),
                                         (cond_high[:, c, at:at + n], cond_low[:, c, at:at + n]))
                products(pe, bank[:, 0:n], terms).then_inc(full, 1)

            def values(u, b, j):
                bank, full = bank_of(f"V{b}{j}", u)
                terms = []
                for c in range(CC):
                    k = slice(b * M + j * P, b * M + j * P + P)
                    terms += split_terms((cond_high[:, c, k], cond_low[:, c, k]),
                                         (wkv_high[:, c, D:], wkv_low[:, c, D:]))
                products(pe, bank[:], terms).then_inc(full, 1)

            def turn_rows(name, u, rows):
                bank, full = bank_of(name, u)
                for c in range(DC):
                    last = pe.transpose(bank[:, c * P:c * P + P], rows[:, c * P:c * P + P], ident[:])
                last.then_inc(full, 1)

            def by_channel(name, u, weights, rows_t):
                bank, full = bank_of(name, u)
                for g in range(HG):
                    w = slice(g * P, g * P + P)
                    last = products(pe, bank[:, w], [(weights[:, c, w], rows_t[:, c, :]) for c in range(DC)])
                last.then_inc(full, 1)

            def by_token(name, u, rows_t, weights):
                bank, full = bank_of(name, u)
                products(pe, bank[:], [(rows_t[:, c, :], weights[:, c, :]) for c in range(DC)]).then_inc(full, 1)

            def small_columns(u):
                bank, full = bank_of("AL", u)
                products(pe, bank[:, 0:H], [(x1n_t[:, c, :], wa[:, c, :]) for c in range(DC)])
                ring.wait_read(pe, "QQ", u)
                for i in range(2):
                    last = products(pe, bank[:, H + H * i:2 * H + H * i],
                                    [(squares[:, i, g * P:g * P + P], head_of[:, g, :]) for g in range(HG)])
                last.then_inc(full, 1)

            def scores(u, b):
                n = u * BU + b
                if not (isinstance(n, int) and n == 0):
                    pe.wait_ge(exp_done, n * HG)
                for g in range(HG):
                    last = pe.matmul(score[:, g, 0:M], q_diag[:, g * BU + b, :], k_t[:, g, b * M:b * M + M],
                                     start=True, stop=True)
                last.then_inc(score_ready, 1)

            def turn_probabilities(u, b):
                n = u * BU + b
                pe.wait_ge(prob_ready, n + 1)
                for j in range(2):
                    for g in range(HG):
                        last = pe.transpose(turned[j][:, g * P:g * P + P], prob[:, g, j * P:j * P + P], ident[:])
                last.then_inc(turned_ready, 1)
                bank, full = bank_of(f"L{b}", u)
                pe.matmul(bank[0:HG, 0:P], prob[:, :, M - 1], ident[:], start=True, stop=True).then_inc(full, 1)

            def attend(u, b):
                n = u * BU + b
                pe.wait_ge(prob_t0_ready, n + 1)
                pe.wait_ge(prob_t1_ready, n + 1)
                ring.wait_read(pe, f"L{b}", u)
                ring.wait_read(pe, f"V{b}1", u)
                if b == 0:
                    pe.wait_ge(v_last_loaded, 16 * u + 16)
                bank, full = bank_of(f"O{b}", u)
                for g in range(HG):
                    w = slice(g * P, g * P + P)
                    last = products(pe, bank[:, w], [(v_s[:, 0, w], prob_t[:, 0, w]), (v_s[:, 1, w], prob_t[:, 1, w]),
                                                     (v_last[:, b, :], prob_last_t[:, g, :])])
                last.then_inc(full, 1)

            def grams(u, b):
                if b == 0:
                    pe.wait_ge(k_diag_ready, u)
                bank, full = bank_of(f"D{b}", u)
                for g in range(HG):
                    i = g * BU + b
                    last = pe.matmul(bank[0:2 * N, g * P:g * P + P], kq[:, i, :], k_diag[:, i, :],
                                     start=True, stop=True)
                last.then_inc(full, 1)

            def turn(u, first=False, last=False):
                a, b_ = not last, not first
                if a:
                    for g in range(4):
                        keys(u, 0, g)
                if b_:
                    pe.wait_ge(x1n_ready, u)
                    turn_rows("X1T", u, x1n)
                if a:
                    keys(u, 1, 0)
                    keys(u, 1, 1)
                if b_:
                    ring.wait_read(pe, "X1T", u)
                    by_channel("KK", u, wattn[:, 1], x1n_t)
                    by_channel("QQ", u, wattn[:, 0], x1n_t)
                if a:
                    keys(u, 1, 2)
                    keys(u, 1, 3)
                    pe.wait_ge(xn_ready, u + 1)
                    turn_rows("XT", u, xn)
                    keys(u, 2, 0)
                    keys(u, 2, 1)
                if b_:
                    by_token("V2", u, x1n_t, wattn[:, 2])
                    by_token("BT", u, x1n_t, wattn[:, 4])
                    by_token("GT", u, x1n_t, wattn[:, 3])
                    small_columns(u)
                if a:
                    keys(u, 2, 2)
                    keys(u, 2, 3)
                    ring.wait_read(pe, "XT", u)
                    by_channel("QT", u, wq, xn_t)
                if b_:
                    for b in range(BU if last else 2):
                        grams(u, b)
                if a:
                    ring.wait_read(pe, "K23", u)
                    pe.wait_ge(q_diag_ready, u + 1)
                    scores(u, 0)
                    values(u, 0, 0)
                    values(u, 0, 1)
                    turn_probabilities(u, 0)
                    for b in range(1, BU):
                        scores(u, b)
                        attend(u, b - 1)
                        values(u, b, 0)
                        values(u, b, 1)
                        turn_probabilities(u, b)
                    if b_:
                        grams(u, 2)
                    attend(u, BU - 1)
                    if b_:
                        grams(u, 3)
                    ring.wait_read(pe, "O3", u)
                    bank, full = bank_of("PR", u)
                    products(pe, bank[:], [(att_t[:, g, :], wproj[:, g, :]) for g in range(HG)]).then_inc(full, 1)

            turn(0, first=True)
            pe.wait_ge(attn_loaded, 16 * 6)
            with pe.Fori(1, NU) as u:
                turn(u)
            turn(NU, last=True)


def time_pass(nc, ident, x1_d, vgb_d, small_d, gram_d, dt_bias, a_log, wo_t, bo, gate_t, expert_t, out):
    with ExitStack() as ctx:
        def sb(name, shape, dt=F32):
            return ctx.enter_context(nc.sbuf_tensor(name, shape, dt))

        def sem(name):
            return ctx.enter_context(nc.semaphore(name))

        experts = sb("experts", [P, E, DC, D])
        wo = sb("wo", [P, DC, D])
        gate = sb("gate", [P, DC, E])
        bo_s = sb("bo_s", [B, D])
        column = sb("column", [B, E])
        ones = sb("ones", [B, H])
        half_off = sb("half_off", [B, H])
        tick = sb("tick2", [B, 1])
        deltas = sb("deltas", [B, N, H, HD])
        decay = sb("decay", [B, H, N])
        alpha = sb("alpha", [B, N, H])
        inv_norm = sb("inv_norm", [B, N, 2 * H])

        with ExitStack() as pre:
            small = pre.enter_context(nc.sbuf_tensor("small_all", [B, N, 3 * H], F32))
            z = pre.enter_context(nc.sbuf_tensor("z", [B, N, H], F32))
            minus_abs = pre.enter_context(nc.sbuf_tensor("minus_abs", [B, N, H], F32))
            log_part = pre.enter_context(nc.sbuf_tensor("log_part", [B, N, H], F32))
            dtb = pre.enter_context(nc.sbuf_tensor("dtb", [B, H], F32))
            alog = pre.enter_context(nc.sbuf_tensor("alog", [B, H], F32))
            rate = pre.enter_context(nc.sbuf_tensor("rate", [B, H], F32))
            loaded = pre.enter_context(nc.semaphore("small_loaded"))
            v_steps = pre.enter_context(nc.semaphore("prepare_vector_steps"))
            a_steps = pre.enter_context(nc.semaphore("prepare_scalar_steps"))
            block = pre.enter_context(nc.Block())

            def over_time(row):
                return row.unsqueeze(1).to_broadcast([B, N, H])

            @block.sync
            def _(sp):
                sp.dma_start(small[:], small_d).then_inc(loaded, 16)
                sp.dma_start(dtb[:], dt_bias.rearrange("(a n) -> a n", a=1).to_broadcast([B, H])).then_inc(loaded, 16)
                sp.dma_start(alog[:], a_log.rearrange("(a n) -> a n", a=1).to_broadcast([B, H])).then_inc(loaded, 16)
                sp.wait_ge(loaded, 48)

            @block.gpsimd
            def _(pool):
                pool.memset(deltas[:], 0.0)
                pool.memset(decay[:], 0.0)
                pool.memset(ones[:], 1.0)
                pool.memset(half_off[:], -0.5)
                for e in range(E):
                    pool.memset(column[:, e:e + 1], float(e))

            @block.vector
            def _(dve):
                dve.wait_ge(loaded, 48)
                dve.tensor_tensor(z[:], small[:, :, 0:H], over_time(dtb[:]), ALU.add).then_inc(v_steps, 1)
                dve.wait_ge(v_steps, 1)
                dve.scalar_tensor_tensor(minus_abs[:], z[:], -1.0, z[:], ALU.mult, ALU.min).then_inc(v_steps, 1)
                dve.wait_ge(a_steps, 3)
                dve.scalar_tensor_tensor(z[:], z[:], 0.0, log_part[:], ALU.max, ALU.add).then_inc(v_steps, 1)
                dve.wait_ge(v_steps, 3)
                dve.tensor_tensor(z[:], z[:], over_time(rate[:]), ALU.mult).then_inc(v_steps, 1)
                dve.wait_ge(a_steps, 5)
                dve.reciprocal(inv_norm[:], small[:, :, H:3 * H]).then_inc(v_steps, 1)
                dve.wait_ge(v_steps, 5)
                dve.tensor_scalar(inv_norm[:, :, H:2 * H], inv_norm[:, :, H:2 * H], SCALE, None, ALU.mult)

            @block.scalar
            def _(act):
                act.wait_ge(v_steps, 2)
                act.activation(minus_abs[:], minus_abs[:], ACT.Exp).then_inc(a_steps, 1)
                act.activation(rate[:], alog[:], ACT.Exp).then_inc(a_steps, 1)
                act.wait_ge(a_steps, 1)
                act.activation(log_part[:], minus_abs[:], ACT.Ln, bias=1.0).then_inc(a_steps, 1)
                act.wait_ge(v_steps, 4)
                act.activation(alpha[:], z[:], ACT.Exp, scale=-1.0).then_inc(a_steps, 1)
                act.activation(small[:, :, H:3 * H], small[:, :, H:3 * H], ACT.Sqrt).then_inc(a_steps, 1)

        x1 = sb("x1_step", [B, D])
        vgb = sb("vgb_slots", [B, 2, 3 * D])
        gram = sb("gram_slots", [B, 2, 2 * D])
        key_row = sb("key_row", [B, H, N])
        query_row = sb("query_row", [B, H, N])
        prod = sb("prod", [B, HD * N])
        pool_prod = sb("pool_prod", [B, 2, HD * N])
        rec = sb("rec", [B, H, HD])
        yv = sb("yv", [B, H, HD])
        ysq = sb("ysq", [B, H, HD])
        mean_sq = sb("mean_sq", [B, H])
        inv_rms = sb("inv_rms", [B, H])
        ctx_t = sb("ctx_t", [P, DC, B])
        x2 = sb("x2", [B, D])
        x2n = sb("x2n", [B, D])
        x2n_t = sb("x2n_t", [P, DC, B])
        acc = sb("acc", [B, D])
        stats = sb("stats2", [B, 6])
        mean_var = sb("mean_var2", [B, 2])
        var_eps = sb("var_eps2", [B, 1])
        rstd = sb("rstd2", [B, 1])
        logits = sb("logits", [B, E])
        best = sb("best", [B, E])
        best_at = sb("best_at", [B, E], U32)
        best_col = sb("best_col", [B, 2])
        lead = sb("lead", [B, 1])
        pair = sb("pair", [B, 2])
        share = sb("share", [B, 2, E])

        mix = ctx.enter_context(nc.psum_tensor("mix", [B, 4, D], F32))
        turn_bank = ctx.enter_context(nc.psum_tensor("turn_bank", [P, DC, B], F32))
        wo_bank = ctx.enter_context(nc.psum_tensor("wo_bank", [B, D], F32))
        logit_bank = ctx.enter_context(nc.psum_tensor("logit_bank", [B, D], F32))

        outputs_loaded, experts_loaded = sem("outputs_loaded"), sem("experts_loaded")
        gram_loaded, vgb_loaded = sem("gram_loaded"), sem("vgb_loaded")
        x1_loaded = sem("x1_step_loaded")
        out_stored = sem("out_stored")
        key_row_ready, query_row_ready = sem("key_row_ready"), sem("query_row_ready")
        delta_ready = sem("delta_ready")
        prod_ready, prod_free = sem("prod_ready"), sem("prod_free")
        y_ready, y_squared = sem("y_ready"), sem("y_squared")
        mean_sq_ready, inv_rms_ready = sem("mean_sq_ready"), sem("inv_rms_ready")
        ctx_ready, ctx_turned, ctx_moved = sem("ctx_ready"), sem("ctx_turned"), sem("ctx_moved")
        wo_ready, x2_done, var_ready, rstd_ready = sem("wo_ready"), sem("x2_done"), sem("var2_ready"), sem("rstd2_ready")
        x2n_ready, x2n_turned, x2n_moved = sem("x2n_ready"), sem("x2n_turned"), sem("x2n_moved")
        logits_ready, logits_read, lead_ready, pair_ready = (sem(n) for n in (
            "logits_ready", "logits_read", "lead_ready", "pair_ready"))
        mix_ready, mix_free = sem("mix_ready"), sem("mix_free")
        combined = sem("combined")
        dve_steps, pool_steps = sem("vector_steps2"), sem("pool_steps2")
        block = ctx.enter_context(nc.Block())

        def slot(tensor, t):
            return tensor[:, bass.ds(t % 2, 1), :].rearrange("b a n -> b (a n)")

        def by_head(row):
            return row.rearrange("b (h e) -> b h e", h=H)

        def each_channel(per_head):
            return per_head.unsqueeze(2).to_broadcast([B, H, HD])

        def heads_of(extent):
            return min(N // extent, 4) if extent <= N // 2 else 1

        def before_outputs(extent):
            return 6 if extent <= N // 4 else 7 if extent <= EARLY else E

        def turns(eng, body, start=None):
            before = 0
            for first, end in ((0, 1), (1, 2), (2, 3), (3, 5), *((a, a + 4) for a in range(5, EARLY, 4)),
                               (EARLY + 1, EARLY + 2), (EARLY + 2, EARLY + 5),
                               *((a, min(a + 4, N - 1)) for a in range(EARLY + 5, N, 4)), (N - 1, N), (N, N + 1), (N + 1, N + 2)):
                extent = min(-(-max(end - 1, 1) // 4) * 4, N)
                stages = (first < N, 1 <= first <= N, first >= 2, first > EARLY + 1)
                n = (SHARED * stages[0] + H * stages[1]) // heads_of(extent)
                with (eng.Fori(first, end) if end - first > 1 else nullcontext(first)) as t:
                    if start:
                        start(t, first, end, extent, stages)
                    body(t, extent, before if end - first == 1 else (t - first) * n + before, stages)
                before += (end - first) * n

        @block.sync
        def _(sp):
            def load_gram(t):
                sp.dma_start(slot(gram, t).rearrange("b (w n) -> b w n", w=2),
                             gram_d[:, :, bass.ds(t, 1), :].rearrange("b w a n -> b w (a n)")).then_inc(gram_loaded, 16)

            def load_vgb(t):
                sp.dma_start(slot(vgb, t), vgb_d[:, bass.ds(t, 1), :].rearrange("b a n -> b (a n)"))\
                    .then_inc(vgb_loaded, 16)

            def load_x1(t):
                sp.dma_start(x1[:], x1_d[:, bass.ds(t, 1), :].rearrange("b a n -> b (a n)")).then_inc(x1_loaded, 16)

            def store(t):
                sp.wait_ge(combined, t + 1)
                sp.dma_start(out[:, bass.ds(t, 1), :].rearrange("b a n -> b (a n)"), acc[:]).then_inc(out_stored, 16)

            load_gram(0)
            load_vgb(0)
            load_x1(0)
            sp.wait_ge(gram_loaded, 16)
            load_gram(1)
            sp.wait_ge(vgb_loaded, 16)
            load_vgb(1)
            for dst, src in ((wo[:], wo_t.rearrange("(c p) n -> p c n", p=P)),
                             (gate[:], gate_t.rearrange("(c p) n -> p c n", p=P)),
                             (bo_s[:], bo.rearrange("(a n) -> a n", a=1).to_broadcast([B, D]))):
                sp.dma_start(dst, src).then_inc(outputs_loaded, 16)
            for e in range(E):
                sp.dma_start(experts[:, e], expert_t[e].rearrange("(c p) n -> p c n", p=P)).then_inc(experts_loaded, 16)
            def turn(t):
                sp.wait_ge(gram_loaded, 16 * t + 16)
                sp.wait_ge(query_row_ready, t)
                load_gram(t + 1)
                sp.wait_ge(vgb_loaded, 16 * t + 16)
                sp.wait_ge(ctx_ready, t)
                load_vgb(t + 1)
                sp.wait_ge(x2_done, t)
                load_x1(t)

            turn(1)
            with sp.Fori(2, N - 1) as t:
                turn(t)
                store(t - 2)
            sp.wait_ge(x2_done, N - 1)
            load_x1(N - 1)
            for t in range(N - 3, N):
                store(t)
            sp.wait_ge(out_stored, 16 * N)

        @block.gpsimd
        def _(pool):
            own = Own(pool, pool_steps)

            def row(dst, t, which, done):
                g = slot(gram, t)[:, which * D:which * D + D].rearrange("b (h s) -> b h s", h=H)
                own.then(pool.tensor_tensor(dst[:], g, decay[:], ALU.mult))
                inv = inv_norm[:, bass.ds(t, 1), which * H:which * H + H].rearrange("b a h -> b h a")
                pool.tensor_tensor(dst[:], dst[:], inv.to_broadcast([B, H, N]), ALU.mult).then_inc(done, 1)

            def products_of(row, first_head, extent, prods, after_two=None):
                nh = heads_of(extent)
                for i, h in enumerate(range(first_head, H, nh)):
                    if not (isinstance(prods, int) and prods + i < 2):
                        pool.wait_ge(prod_free, prods + i - 1)
                    p = pool_prod[:, i % 2, 0:nh * HD * extent].rearrange("b (s h e) -> b s h e", h=nh, e=HD)
                    c = row[:, h:h + nh, 0:extent].rearrange("b h s -> b s h").unsqueeze(3)
                    pool.tensor_tensor(p, c.to_broadcast([B, extent, nh, HD]), deltas[:, 0:extent, h:h + nh, :],
                                       ALU.mult).then_inc(prod_ready, 1)
                    if i == 1 and after_two:
                        after_two()
                return prods + (H - first_head) // nh

            def decay_to(t):
                a = alpha[:, bass.ds(t, 1), :].rearrange("b a h -> b h a").to_broadcast([B, H, N])
                own.then(pool.tensor_tensor(decay[:], decay[:], a, ALU.mult))

            def body(t, extent, prods, stages):
                deltas_stage, outputs_stage, mix_stage, _ = stages

                def norm_power():
                    pool.wait_ge(var_ready, t - 1)
                    pool.tensor_tensor(rstd[:], var_eps[:], half_off[:, 0:1], ALU.pow).then_inc(rstd_ready, 1)

                if deltas_stage:
                    if isinstance(t, int) and t == 0:
                        decay_to(0)
                    pool.wait_ge(gram_loaded, 16 * t + 16)
                    if outputs_stage:
                        pool.wait_ge(delta_ready, t)
                    row(key_row, t, 0, key_row_ready)
                    own.then(pool.tensor_copy(decay[:, :, bass.ds(t, 1)], ones[:].unsqueeze(2)))
                    pool.wait_ge(key_row_ready, t + 1)
                    prods = products_of(key_row, H - SHARED, extent, prods, norm_power if mix_stage else None)
                elif mix_stage:
                    norm_power()
                if outputs_stage:
                    pool.wait_ge(delta_ready, t)
                    pool.wait_ge(query_row_ready, t)
                    prods = products_of(query_row, 0, extent, prods)
                if deltas_stage:
                    if outputs_stage:
                        pool.wait_ge(prod_ready, prods)
                    row(query_row, t, 1, query_row_ready)
                    if not (isinstance(t, int) and t == N - 1):
                        pool.wait_ge(query_row_ready, t + 1)
                        decay_to(t + 1)
                if outputs_stage:
                    pool.wait_ge(mean_sq_ready, t)
                    pool.tensor_tensor(inv_rms[:], mean_sq[:], half_off[:], ALU.pow).then_inc(inv_rms_ready, 1)

            def start(t, first, end, extent, stages):
                own.turn(1, t, 4) if first > 0 else own.turn(0, 0, 0)

            turns(pool, body, start)

        @block.scalar
        def _(act):
            def body(t, extent, prods, stages):
                _, outputs_stage, mix_stage, _ = stages
                if mix_stage:
                    act.wait_ge(x2n_turned, t - 1)
                    act.activation(x2n_t[:], turn_bank[:], ACT.Copy).then_inc(x2n_moved, 1)
                    act.wait_ge(lead_ready, t - 1)
                    act.activation(pair[:, 0:1], lead[:], ACT.Sigmoid)
                    act.activation(pair[:, 1:2], lead[:], ACT.Sigmoid, scale=-1.0).then_inc(pair_ready, 1)
                if outputs_stage:
                    act.wait_ge(y_ready, t)
                    act.activation(ysq[:], yv[:], ACT.Square).then_inc(y_squared, 1)
                    act.wait_ge(ctx_turned, t)
                    act.activation(ctx_t[:], turn_bank[:], ACT.Copy).then_inc(ctx_moved, 1)

            turns(act, body)

        @block.vector
        def _(dve):
            own = Own(dve, dve_steps, lambda: dve.tensor_copy(tick[:], half_off[:, 0:1]))

            used = {}

            def own_product(extent, h):
                nh = heads_of(extent)
                p = prod[:, 0:nh * HD * extent].rearrange("b (h e s) -> b h e s", h=nh, e=HD)
                c = key_row[:, h:h + nh, 0:extent].unsqueeze(2).to_broadcast([B, nh, HD, extent])
                d = deltas[:, 0:extent, h:h + nh, :].rearrange("b s h e -> b h e s")
                if "summed" in used:
                    own.wait(used["summed"])
                used["made"] = own.did(dve.tensor_tensor(p, c, d, ALU.mult))

            def own_sum(extent, h):
                nh = heads_of(extent)
                p = prod[:, 0:nh * HD * extent].rearrange("b (h e s) -> b h e s", h=nh, e=HD)
                own.wait(used["made"])
                used["summed"] = own.did(dve.tensor_reduce(rec[:, h:h + nh, :], p, AX.X, ALU.add))

            def pool_sum(dst, extent, h, i, count):
                nh = heads_of(extent)
                dve.wait_ge(prod_ready, count)
                p = pool_prod[:, i % 2, 0:nh * HD * extent].rearrange("b (s h e) -> b h e s", h=nh, e=HD)
                dve.tensor_reduce(dst[:, h:h + nh, :], p, AX.X, ALU.add).then_inc(prod_free, 1)

            def solve(t, outputs_stage, sums):
                dve.wait_ge(prod_free, sums)
                dve.wait_ge(vgb_loaded, 16 * t + 16)
                own.wait(used.pop("summed"))
                own.then(dve.tensor_tensor(rec[:], by_head(slot(vgb, t)[:, 0:D]), rec[:], ALU.subtract))
                own.then(dve.tensor_tensor(rec[:], rec[:], by_head(slot(vgb, t)[:, 2 * D:]), ALU.mult))
                inv = inv_norm[:, bass.ds(t, 1), 0:H].rearrange("b a h -> b h a")
                if outputs_stage:
                    dve.wait_ge(query_row_ready, t + 1)
                dve.tensor_tensor(deltas[:, bass.ds(t, 1)].rearrange("b a h e -> b (a h) e"), rec[:],
                                  inv.to_broadcast([B, H, HD]), ALU.mult).then_inc(delta_ready, 1)

            def mean_square(t):
                dve.wait_ge(y_squared, t + 1)
                own.then(dve.tensor_reduce(mean_sq[:], ysq[:], AX.X, ALU.add))
                dve.tensor_scalar(mean_sq[:], mean_sq[:], 1.0 / HD, RMS_EPS, ALU.mult, ALU.add).then_inc(mean_sq_ready, 1)

            def gated(t):
                own.then(dve.tensor_tensor(yv[:], yv[:], by_head(slot(vgb, t)[:, D:2 * D]), ALU.mult))
                dve.wait_ge(inv_rms_ready, t + 1)
                dve.tensor_tensor(ysq[:], yv[:], each_channel(inv_rms[:]), ALU.mult).then_inc(ctx_ready, 1)

            def residual(t):
                dve.wait_ge(x1_loaded, 16 * t + 16)
                dve.wait_ge(wo_ready, t + 1)
                dve.tensor_tensor(x2[:], wo_bank[:], x1[:], ALU.add).then_inc(x2_done, 1)
                dve.wait_ge(x2_done, t + 1)
                own.then(dve.tensor_tensor(x2[:], x2[:], bo_s[:], ALU.add))
                own.then_apart(dve.bn_stats(stats[:], x2[:]))
                own.then(dve.bn_aggr(mean_var[:], stats[:]))
                dve.tensor_scalar(var_eps[:], mean_var[:, 1:2], LN_EPS, None, ALU.add).then_inc(var_ready, 1)

            def normed(t):
                dve.wait_ge(rstd_ready, t + 1)
                dve.tensor_scalar(x2n[:], x2[:], mean_var[:, 0:1], rstd[:], ALU.subtract, ALU.mult)\
                    .then_inc(x2n_ready, 1)

            def route(t):
                dve.wait_ge(logits_ready, t + 1)
                dve.tensor_copy(logits[:], logit_bank[:, 0:E]).then_inc(logits_read, 1)
                wait_apart(dve, logits_read, t + 1)
                own.then(dve.max(best[:], logits[:]))
                dve.tensor_tensor(lead[:], best[:, 0:1], best[:, 1:2], ALU.subtract).then_inc(lead_ready, 1)
                own.then(dve.max_index(best_at[:], best[:], logits[:]))
                own.then(dve.tensor_copy(best_col[:], best_at[:, 0:2]))

            def shares(t):
                dve.wait_ge(pair_ready, t + 1)
                for i in range(2):
                    c = own.did(dve.tensor_scalar(share[:, i, :], column[:], best_col[:, i:i + 1], pair[:, i:i + 1],
                                                  ALU.is_equal, ALU.mult))
                own.wait(c)
                own.then(dve.tensor_tensor(share[:, 0, :], share[:, 0, :], share[:, 1, :], ALU.add))

            def combine(t, e):
                dve.wait_ge(mix_ready, 8 * t + e + 1)
                if e == 0 and not (isinstance(t, int) and t == 0):
                    dve.wait_ge(out_stored, 16 * t)
                if e > 0:
                    dve.wait_ge(mix_free, 7 * t + e)
                dve.scalar_tensor_tensor(acc[:], mix[:, e % 4, :], share[:, 0, e:e + 1], x2[:] if e == 0 else acc[:],
                                         ALU.mult, ALU.add).then_inc(combined if e == E - 1 else mix_free, 1)

            def body(t, extent, prods, stages):
                deltas_stage, outputs_stage, mix_stage, _ = stages
                nh = heads_of(extent)
                theirs, count, mine, later = [], prods, [], []
                if deltas_stage:
                    for i, h in enumerate(range(H - SHARED, H, nh)):
                        theirs.append(lambda h=h, i=i, c=count: pool_sum(rec, extent, h, i, c + i + 1))
                    count = count + SHARED // nh
                    for h in range(0, H - SHARED, nh):
                        mine += [lambda h=h: own_product(extent, h), lambda h=h: own_sum(extent, h)]
                    dve.wait_ge(key_row_ready, t + 1)
                    for _ in range(4 if stages[3] else 2):
                        mine.pop(0)()
                k = before_outputs(extent)
                if stages[3]:
                    combine(t - 3, 7)
                    residual(t - 2)
                    later.append(lambda: normed(t - 2))
                if mix_stage:
                    later.append(lambda: (route(t - 2), shares(t - 2)))
                    later += [lambda e=e: combine(t - 2, e) for e in range(k - 2)]
                if outputs_stage:
                    for i, h in enumerate(range(0, H, nh)):
                        theirs.append(lambda h=h, i=i, c=count: pool_sum(yv, extent, h, i, c + i + 1))
                    count = count + H // nh
                for task in merged(theirs, merged(mine, later)):
                    task()
                if outputs_stage:
                    dve.wait_ge(prod_free, count)
                    dve.tensor_copy(tick[:], half_off[:, 0:1]).then_inc(y_ready, 1)
                if mix_stage:
                    combine(t - 2, k - 2)
                if outputs_stage:
                    mean_square(t - 1)
                if deltas_stage:
                    solve(t, outputs_stage, count)
                if outputs_stage:
                    gated(t - 1)
                ends_with_residual = extent <= EARLY and outputs_stage
                if mix_stage:
                    for e in range(k - 1, 8):
                        if ends_with_residual and e == k:
                            residual(t - 1)
                        if ends_with_residual and e == 7:
                            normed(t - 1)
                        if e < 7 or extent <= EARLY or (isinstance(t, int) and t == N + 1):
                            combine(t - 2, e)
                elif ends_with_residual:
                    residual(t - 1)
                    normed(t - 1)

            def own_steps(extent, stages):
                deltas_stage, outputs_stage, mix_stage, _ = stages
                return (2 * ((H - SHARED) // heads_of(extent)) + 2) * deltas_stage \
                    + 2 * outputs_stage + 6 * mix_stage \
                    + 4 * ((extent <= EARLY and outputs_stage) + stages[3])

            counted = {"before": 0, "turn": None}

            def start(t, first, end, extent, stages):
                if counted["turn"] is not None:
                    n, per_turn = counted["turn"]
                    assert own.n == per_turn, (own.n, per_turn)
                    counted["before"] += n * per_turn
                per_turn = own_steps(extent, stages)
                n = end - first
                counted["turn"] = (n, per_turn)
                own.turn(counted["before"], t - first, per_turn)

            dve.wait_ge(outputs_loaded, 48)
            turns(dve, body, start)

        @block.tensor
        def _(pe):
            def mix_expert(t, e):
                if e >= 4:
                    pe.wait_ge(mix_free, 7 * t + e - 3)
                elif not (isinstance(t, int) and t == 0):
                    if e < 3:
                        pe.wait_ge(mix_free, 7 * t + e - 2)
                    else:
                        pe.wait_ge(combined, t)
                products(pe, mix[:, e % 4, :], [(x2n_t[:, c, :], experts[:, e, c, :]) for c in range(DC)])\
                    .then_inc(mix_ready, 1)

            def turn_rows(rows, done):
                for c in range(DC):
                    last = pe.transpose(turn_bank[:, c, :], rows[:, c * P:c * P + P], ident[0:B, 0:B])
                last.then_inc(done, 1)

            def body(t, extent, prods, stages):
                _, outputs_stage, mix_stage, _ = stages
                k = before_outputs(extent)
                if isinstance(t, int) and t == 1:
                    pe.wait_ge(outputs_loaded, 48)
                if isinstance(t, int) and t == 2:
                    pe.wait_ge(experts_loaded, 16 * E)
                if mix_stage:
                    pe.wait_ge(x2n_ready, t - 1)
                    turn_rows(x2n, x2n_turned)
                    pe.wait_ge(x2n_moved, t - 1)
                    if not (isinstance(t, int) and t == 2):
                        pe.wait_ge(logits_read, t - 2)
                    products(pe, logit_bank[:, 0:E], [(x2n_t[:, c, :], gate[:, c, :]) for c in range(DC)])\
                        .then_inc(logits_ready, 1)
                    for e in range(k):
                        mix_expert(t - 2, e)
                if outputs_stage:
                    pe.wait_ge(ctx_ready, t)
                    turn_rows(ysq[:].rearrange("b h e -> b (h e)"), ctx_turned)
                    pe.wait_ge(ctx_moved, t)
                    if not (isinstance(t, int) and t == 1):
                        pe.wait_ge(x2_done, t - 1)
                    products(pe, wo_bank[:], [(ctx_t[:, c, :], wo[:, c, :]) for c in range(DC)]).then_inc(wo_ready, 1)
                if mix_stage:
                    for e in range(k, E):
                        mix_expert(t - 2, e)

            turns(pe, body)


INPUTS = ["x", "cond_t", "cond_last_t", "q_w", "q_b", "kv_w", "kv_b", "proj_w", "proj_b", "attn_w_t", "wa_t",
          "dt_bias", "a_log", "norm_w", "wo_t", "bo", "gate_t", "expert_t"]


def laid_out(x, ctx_768, L0_xattn_q_w, L0_xattn_q_b, L0_xattn_kv_w, L0_xattn_kv_b, L0_xattn_proj_w, L0_xattn_proj_b,
             L0_attn_Wq, L0_attn_Wk, L0_attn_Wv, L0_attn_Wg, L0_attn_Wb, L0_attn_Wa, L0_attn_dt_bias, L0_attn_A_log,
             L0_attn_norm_w, L0_attn_Wo, L0_attn_bo, L0_ffn_gate_w, L0_ffn_expert_w):
    import numpy as np

    ctx = np.asarray(ctx_768)
    arrays = [x, ctx.transpose(2, 0, 1).reshape(C, B * M), ctx[:, M - 1, :].T, L0_xattn_q_w,
              np.asarray(L0_xattn_q_b).reshape(-1, P).T, L0_xattn_kv_w,
              np.asarray(L0_xattn_kv_b).reshape(-1, P).T, L0_xattn_proj_w, L0_xattn_proj_b,
              np.stack([np.asarray(w).T for w in (L0_attn_Wq, L0_attn_Wk, L0_attn_Wv, L0_attn_Wg, L0_attn_Wb)]),
              np.asarray(L0_attn_Wa).T, L0_attn_dt_bias, L0_attn_A_log, L0_attn_norm_w, np.asarray(L0_attn_Wo).T,
              L0_attn_bo, np.asarray(L0_ffn_gate_w).T, np.asarray(L0_ffn_expert_w).transpose(0, 2, 1)]
    return {name: np.ascontiguousarray(a) for name, a in zip(INPUTS, arrays)}


def kernel(**inputs):
    import concourse.bacc as bacc
    from concourse.bass_utils import run_bass_kernel_spmd

    arrays = laid_out(**inputs)
    nc = bacc.Bacc("TRN2", target_bir_lowering=False, num_devices=1)
    args = [nc.dram_tensor(f"{name}_dram", a.shape, mybir.dt.from_np(a.dtype), kind="ExternalInput").ap()
            for name, a in arrays.items()]
    out = nc.dram_tensor("out", [B, N, D], F32, kind="ExternalOutput").ap()
    build(nc, *args, out)
    result = run_bass_kernel_spmd(nc, [{f"{name}_dram": a for name, a in arrays.items()}], core_ids=[0])
    return result.results[0]["out"]
```
